# Optimizing a Trainium2 kernel written in Bass

```python
import numpy as np
import jax
import jax.numpy as jnp

def _softmax(x, axis=-1):
    return jax.nn.softmax(x, axis=axis)

def _gelu(x):
    return jax.nn.gelu(x, approximate=True)

def _silu(x):
    return jax.nn.silu(x)

def _sigmoid(x):
    return jax.nn.sigmoid(x)

def _layernorm(x, axis=-1, eps=1e-05):
    m = jnp.mean(x, axis=axis, keepdims=True)
    v = jnp.var(x, axis=axis, keepdims=True)
    return (x - m) / jnp.sqrt(v + eps)

def _scatter_add(tgt, idx, src, axis=0):
    return tgt.at[idx].add(src)

def _segment_sum(src, seg, n):
    return jax.ops.segment_sum(src, seg, n)
kernel_name = 'mk_adaln_d1_jaxref_r8_b180de'

def setup_inputs(seed: int=0):
    np.random.seed(seed)
    _w = jnp.asarray

    def _L0_attn_setup():
        import jax, jax.numpy as jnp
        import numpy as np
        EMBED_DIM = 128
        NUM_HEADS = 16
        HEAD_DIM = EMBED_DIM // NUM_HEADS
        WINDOW = 128
        key = jax.random.key(seed)
        ks = jax.random.split(key, 9)
        B, S, E = (4, 512, EMBED_DIM)
        s = 1.0 / np.sqrt(E)
        return {'x': jax.random.normal(ks[0], (B, S, E), jnp.float32), 'Wq': jax.random.normal(ks[1], (E, E), jnp.float32) * s, 'bq': jnp.zeros((E,), jnp.float32), 'Wk': jax.random.normal(ks[2], (E, E), jnp.float32) * s, 'bk': jnp.zeros((E,), jnp.float32), 'Wv': jax.random.normal(ks[3], (E, E), jnp.float32) * s, 'bv': jnp.zeros((E,), jnp.float32), 'Wo': jax.random.normal(ks[4], (E, E), jnp.float32) * s, 'bo': jnp.zeros((E,), jnp.float32)}
    _L0_attn_in = _L0_attn_setup()

    def _L0_ffn_setup():
        import jax, jax.numpy as jnp
        import numpy as np
        DIM = 128

        def _reference_tuple_inner(x, W_r, W_k, W_v, mu_r, mu_k):
            B, T, C = x.shape
            x_prev = jnp.concatenate([jnp.zeros((B, 1, C), x.dtype), x[:, :-1, :]], axis=1)
            xr = mu_r * x + (1.0 - mu_r) * x_prev
            xk = mu_k * x + (1.0 - mu_k) * x_prev
            r = jax.nn.sigmoid(jnp.einsum('btc,dc->btd', xr, W_r))
            k = jnp.einsum('btc,dc->btd', xk, W_k)
            k_act = jnp.square(jax.nn.relu(k))
            out = r * jnp.einsum('btc,dc->btd', k_act, W_v)
            new_state = x[:, -1, :]
            return (out, new_state)
        key = jax.random.key(seed)
        ks = jax.random.split(key, 6)
        B, T, C = (8, 256, DIM)
        x = jax.random.normal(ks[0], (B, T, C), dtype=jnp.float32)
        s = 1.0 / np.sqrt(C)
        W_r = jax.random.uniform(ks[1], (C, C), jnp.float32, -s, s)
        W_k = jax.random.uniform(ks[2], (C, C), jnp.float32, -s, s)
        W_v = jax.random.uniform(ks[3], (C, C), jnp.float32, -s, s)
        mu_r = jax.random.uniform(ks[4], (C,), jnp.float32)
        mu_k = jax.random.uniform(ks[5], (C,), jnp.float32)
        return {'x': x, 'W_r': W_r, 'W_k': W_k, 'W_v': W_v, 'mu_r': mu_r, 'mu_k': mu_k}
    _L0_ffn_in = _L0_ffn_setup()
    _L0_c = _w((lambda *s: np.random.randn(*s).astype(np.float32) * 0.05)(4, 128))
    _L0_wmod = _w((lambda *s: np.random.randn(*s).astype(np.float32) * 0.05)(128, 6 * 128) * 128 ** (-0.5))
    _d = {'L0_attn_x': _L0_attn_in['x'], 'L0_attn_Wq': _L0_attn_in['Wq'], 'L0_attn_bq': _L0_attn_in['bq'], 'L0_attn_Wk': _L0_attn_in['Wk'], 'L0_attn_bk': _L0_attn_in['bk'], 'L0_attn_Wv': _L0_attn_in['Wv'], 'L0_attn_bv': _L0_attn_in['bv'], 'L0_attn_Wo': _L0_attn_in['Wo'], 'L0_attn_bo': _L0_attn_in['bo'], 'L0_ffn_W_r': _L0_ffn_in['W_r'], 'L0_ffn_W_k': _L0_ffn_in['W_k'], 'L0_ffn_W_v': _L0_ffn_in['W_v'], 'L0_ffn_mu_r': _L0_ffn_in['mu_r'], 'L0_ffn_mu_k': _L0_ffn_in['mu_k'], 'L0_c': _L0_c, 'L0_wmod': _L0_wmod}
    _x0 = _d['L0_attn_x']
    _d['L0_attn_x'] = jax.random.normal(jax.random.fold_in(jax.random.key(seed), 1), (4, 512, 128), dtype=_x0.dtype)
    del _x0
    return _d

def reference(L0_attn_x, L0_attn_Wq, L0_attn_bq, L0_attn_Wk, L0_attn_bk, L0_attn_Wv, L0_attn_bv, L0_attn_Wo, L0_attn_bo, L0_ffn_W_r, L0_ffn_W_k, L0_ffn_W_v, L0_ffn_mu_r, L0_ffn_mu_k, L0_c, L0_wmod):

    def _L0_attn_ref(x, Wq, bq, Wk, bk, Wv, bv, Wo, bo):
        import jax, jax.numpy as jnp
        import numpy as np
        EMBED_DIM = 128
        NUM_HEADS = 16
        HEAD_DIM = EMBED_DIM // NUM_HEADS
        WINDOW = 128
        B, S, E = x.shape
        H, D, W = (NUM_HEADS, HEAD_DIM, WINDOW)
        scale = jnp.sqrt(jnp.asarray(D, x.dtype))

        def heads(t):
            return t.reshape(B, S, H, D).transpose(0, 2, 1, 3)
        q = heads(x @ Wq + bq)
        k = heads(x @ Wk + bk)
        v = heads(x @ Wv + bv)
        offs = jnp.arange(-W, W + 1)
        idx = jnp.arange(S)[:, None] + offs[None, :]
        valid = (idx >= 0) & (idx < S)
        idxc = jnp.clip(idx, 0, S - 1)
        k_win = k[:, :, idxc, :]
        v_win = v[:, :, idxc, :]
        scores = jnp.einsum('bhsd,bhswd->bhsw', q, k_win) / scale
        scores = jnp.where(valid[None, None], scores, jnp.asarray(-jnp.inf, scores.dtype))
        attn = jax.nn.softmax(scores, axis=-1)
        out = jnp.einsum('bhsw,bhswd->bhsd', attn, v_win)
        out = out.transpose(0, 2, 1, 3).reshape(B, S, E)
        return out @ Wo + bo

    def _L0_ffn_ref(x, W_r, W_k, W_v, mu_r, mu_k):
        import jax, jax.numpy as jnp
        import numpy as np
        DIM = 128

        def _reference_tuple_inner(x, W_r, W_k, W_v, mu_r, mu_k):
            B, T, C = x.shape
            x_prev = jnp.concatenate([jnp.zeros((B, 1, C), x.dtype), x[:, :-1, :]], axis=1)
            xr = mu_r * x + (1.0 - mu_r) * x_prev
            xk = mu_k * x + (1.0 - mu_k) * x_prev
            r = jax.nn.sigmoid(jnp.einsum('btc,dc->btd', xr, W_r))
            k = jnp.einsum('btc,dc->btd', xk, W_k)
            k_act = jnp.square(jax.nn.relu(k))
            out = r * jnp.einsum('btc,dc->btd', k_act, W_v)
            new_state = x[:, -1, :]
            return (out, new_state)
        return _reference_tuple_inner(x, W_r, W_k, W_v, mu_r, mu_k)[0]
    x = L0_attn_x
    mod = (_silu(L0_c) @ L0_wmod).reshape(L0_c.shape[0], 6, 1, -1)
    sa, ca, ga, sb, cb, gb = (mod[:, 0], mod[:, 1], mod[:, 2], mod[:, 3], mod[:, 4], mod[:, 5])
    ga = (2 * (ga >= 0) - 1) * jnp.maximum(jnp.abs(ga), 0.25)
    gb = (2 * (gb >= 0) - 1) * jnp.maximum(jnp.abs(gb), 0.25)
    h = _layernorm(x, axis=-1) * (1 + ca) + sa
    x = x + ga * _L0_attn_ref(h, L0_attn_Wq, L0_attn_bq, L0_attn_Wk, L0_attn_bk, L0_attn_Wv, L0_attn_bv, L0_attn_Wo, L0_attn_bo)
    h = _layernorm(x, axis=-1) * (1 + cb) + sb
    x = x + gb * _L0_ffn_ref(h, L0_ffn_W_r, L0_ffn_W_k, L0_ffn_W_v, L0_ffn_mu_r, L0_ffn_mu_k)
    return x

_drawn_inputs = setup_inputs


def setup_inputs(seed=0):
    import zlib

    import numpy as np

    out = dict(_drawn_inputs(seed))
    spreads = {'L0_attn_bq': (0.0, 0.8),
     'L0_attn_bk': (0.0, 0.8),
     'L0_attn_bv': (0.0, 0.341),
     'L0_attn_bo': (0.0, 0.324)}
    factors = {'L0_ffn_W_r': 8.0,
     'L0_ffn_W_k': 2.968,
     'L0_ffn_W_v': 2.753,
     'L0_ffn_mu_r': 8.0,
     'L0_ffn_mu_k': 4.653}
    for name, (base, spread) in spreads.items():
        noise = np.random.default_rng([zlib.crc32(name.encode()), seed]).standard_normal(out[name].shape)
        drawn = base * np.exp(spread * noise) if base else spread * noise
        out[name] = jnp.asarray(drawn.astype(out[name].dtype))
    for name, factor in factors.items():
        out[name] = (out[name] * factor).astype(out[name].dtype)
    return out
```

```python
from contextlib import ExitStack

import numpy as np

import concourse.bass as bass
from concourse import mybir

F32 = mybir.dt.float32
BF16 = mybir.dt.bfloat16
ACT = mybir.ActivationFunctionType
ALU = mybir.AluOpType
AX = mybir.AxisListType

P = 128
EPS = 1e-5
GATE_FLOOR = 0.25
MASKED = -1e30
ONES = float(np.array([0x3F803F80], np.uint32).view(np.float32)[0])


def adaln_block(nc, x, Wq, bq, Wk, bk, Wv, bv, Wo, bo, W_r, W_k, W_v, mu_r, mu_k, c, wmod, out):
    B, S, E = x.shape
    D = 8
    NT = S // P
    BLK = 64
    NB = S // BLK
    REACH = P // BLK
    WIN = 2 * REACH + 1
    PAIRS = E // D // 2
    GP = 4
    NG = PAIRS // GP
    STEPS = B * NG * NB
    PARTS = 3
    PRODUCTS = [(0, 0), (0, 1), (1, 0), (1, 1), (0, 2), (2, 0)]
    ROWS = len(PRODUCTS) * D
    KBUF = 3
    VW = 32
    assert E == P and S % P == 0 and NG * GP == PAIRS and GP * VW == P

    ctx = ExitStack()
    with ctx:
        def sb(name, shape, dt=F32):
            return ctx.enter_context(nc.sbuf_tensor(name, shape, dt))

        def sem(name):
            return ctx.enter_context(nc.semaphore(name))

        pe, dve, act, pool, sp = nc.tensor, nc.vector, nc.scalar, nc.gpsimd, nc.sync

        s_pe, s_dve, s_act, s_pool = sem("s_pe"), sem("s_dve"), sem("s_act"), sem("s_pool")
        count, seen = {}, {}

        def done(instruction, semaphore, by=1):
            instruction.then_inc(semaphore, by)
            count[id(semaphore)] = count.get(id(semaphore), 0) + by
            return semaphore, count[id(semaphore)]

        def wait(engine, *events):
            for event in events:
                if event is None:
                    continue
                semaphore, value = event
                key = (id(engine), id(semaphore))
                if seen.get(key, 0) < value:
                    engine.wait_ge(semaphore, value)
                    seen[key] = value

        def by_pe(i):
            return done(i, s_pe)

        def by_dve(i):
            return done(i, s_dve)

        def by_act(i):
            return done(i, s_act)

        def by_pool(i):
            return done(i, s_pool)

        pool_start = [0]

        def pool_from(partition):
            if pool_start[0] != partition:
                wait(pool, (s_pool, count[id(s_pool)]))
                pool_start[0] = partition

        xt = sb("xt", [P, B * NT, E])
        w_in = sb("w_in", [P, 7, E])
        wqk = sb("wqk", [P, 2, E])
        wT = sb("wT", [P, 3, E])
        wo_gated = sb("wo_gated", [P, B, E])
        wv_gated = sb("wv_gated", [P, B, E])
        wmod_sb = sb("wmod_sb", [P, 6 * E])
        cols = sb("cols", [P, 5])
        bq_scaled = sb("bq_scaled", [P, 1])
        bo_row = sb("bo_row", [1, E])
        ones_row = sb("ones_row", [1, P])
        c_sb = sb("c_sb", [B, E])
        c_tmp = sb("c_tmp", [B, 3, E])
        siluT = sb("siluT", [P, B])
        silu_wide = sb("silu_wide", [P, B, P])
        modT = sb("modT", [P, 4, B])
        gates = sb("gates", [P, B, 2, E])
        bo_gated = sb("bo_gated", [P, B, E])
        identF = sb("identF", [P, P])
        identB = sb("identB", [P, P], BF16)
        band = sb("band", [P, 4, BLK], BF16)
        half = sb("half", [P, NT])

        stats = sb("stats", [P, NT, 6])
        mean_var = sb("mean_var", [P, NT, 2])
        var_eps = sb("var_eps", [P, NT])
        rstd = sb("rstd", [P, NT])
        xn = sb("xn", [P, NT, E])
        hT = sb("hT", [P, S])
        qk32 = sb("qk32", [P, 2, S])
        qk_rest = sb("qk_rest", [P, 2, S])
        qk_parts = sb("qk_parts", [P, 2, PARTS, S], BF16)
        q_ops = [sb(f"q_ops{b}", [P, PAIRS, S], BF16) for b in range(B)]
        k_ops = [sb(f"k_ops{b}", [P, 2, PAIRS, S], BF16) for b in range(KBUF)]
        vals = [sb(f"vals{b}", [P, NB, PAIRS, VW]) for b in range(KBUF)]
        neg_max = sb("neg_max", [P, 2, 2, GP, NB // 2])
        max_rest = sb("max_rest", [P, 2, GP * NB // 2])
        max_parts = sb("max_parts", [P, 2, PARTS, GP * NB // 2], BF16)
        max_rows = sb("max_rows", [2 * PARTS * GP * NB // 2, 2, P], BF16)
        RING = 4
        probs = sb("probs", [P, RING, GP, WIN * BLK])
        sums_T = sb("sums_T", [P, 2, S])
        inv = sb("inv", [P, 2, NT, 2 * GP])
        o_tok = sb("o_tok", [P, NT, E])
        o_T = sb("o_T", [P, S])
        h2 = sb("h2", [P, 1 + S])
        h2_diff = sb("h2_diff", [P, S])
        mixed = sb("mixed", [P, 2, S])
        gate_r = sb("gate_r", [P, NT, E])
        k_relu = sb("k_relu", [P, S])
        k_sq = sb("k_sq", [P, S])
        y2 = sb("y2", [P, NT, E])

        ps_work = ctx.enter_context(nc.psum_tensor("ps_work", [P, 2, 2, 512], F32))
        ps_exp = ctx.enter_context(nc.psum_tensor("ps_exp", [P, 3, 512], F32))
        ps_sum = ctx.enter_context(nc.psum_tensor("ps_sum", [P, 512], F32))

        s_x = [sem(f"s_x{b}") for b in range(B)]
        s_w, s_small, s_out = sem("s_w"), sem("s_small"), sem("s_out")
        s_ops = [sem(f"s_ops{b}") for b in range(B)]
        s_max = [sem(f"s_max{n}") for n in range(B * NG)]

        def load_x(b):
            return done(sp.dma_start(xt[:, NT * b:NT * (b + 1), :], x[b].rearrange("(t p) e -> p t e", p=P)), s_x[b], 16)

        x_in = {0: load_x(0)}
        small = done(sp.dma_start(c_sb[:, :], c), s_small, 16)
        weights = done(sp.dma_start(wmod_sb[:, :], wmod), s_w, 16)
        for n, w in enumerate((Wq, Wk, Wv, Wo, W_r, W_k, W_v)):
            weights = done((sp if n < 3 else act).dma_start(w_in[:, n, :], w), s_w, 16)
        with nc.allow_non_contiguous_dma(reason="bias columns, 128 elements each"):
            for n, v in enumerate((bq, bk)):
                for m in range(2):
                    small = done(act.dma_start(cols[BLK * m:BLK * (m + 1), n:n + 1],
                                               v.rearrange("(p m d) -> m d p", m=2, d=D)[m]), s_small, 16)
            for n, v in enumerate((bv, mu_r, mu_k)):
                small = done(act.dma_start(cols[:, 2 + n:3 + n], v.rearrange("(p a) -> p a", a=1)), s_small, 16)
        small = done(sp.dma_start(bo_row[:, :], bo.rearrange("(a d) -> a d", a=1)), s_small, 16)
        for b in range(1, B):
            x_in[b] = load_x(b)

        zeroed = by_pool(pool.memset(identF[:, :], 0.0))
        zeroed = by_pool(pool.memset(band[:, :, :], 0.0))
        by_pool(pool.memset(half[:, :], -0.5))
        wait(pool, zeroed)
        pool_from(0)
        identF_ok = by_pool(pool.affine_select(out=identF[:, :], in_=identF[:, :], compare_op=ALU.not_equal, fill=1.0,
                                               base=0, pattern=[[-1, P]], channel_multiplier=1))
        for m in range(2):
            rows = slice(BLK * m, BLK * (m + 1))
            pool_from(BLK * m)
            by_pool(pool.affine_select(out=band[rows, 1, :], in_=band[rows, 1, :], compare_op=ALU.is_ge, fill=MASKED,
                                       base=0, pattern=[[1, BLK]], channel_multiplier=-1))
            by_pool(pool.affine_select(out=band[rows, 2, :], in_=band[rows, 2, :], compare_op=ALU.is_ge,
                                       fill=MASKED, base=0, pattern=[[-1, BLK]], channel_multiplier=1))
            band_ok = by_pool(pool.memset(band[rows, 3 * m, :], MASKED))
        wait(dve, identF_ok)
        identB_ok = by_dve(dve.tensor_copy(identB[:, :], identF[:, :]))
        q_clear, k_clear = {}, {}

        def words(t):
            return t.rearrange("p a s -> p (a s)").bitcast(F32)

        ones_set = by_dve(dve.memset(ones_row[:, :], 1.0))
        for b in range(B):
            q_clear[b] = by_dve(dve.memset(words(q_ops[b][:, :, :]), 0.0))
            if b < KBUF:
                for m in range(2):
                    h = slice(BLK * m, BLK * (m + 1))
                    by_dve(dve.memset(words(k_ops[b][h, m, :, :]), ONES))
                    k_clear[b] = by_dve(dve.memset(words(k_ops[b][h, 1 - m, :, :]), 0.0))
            pool_from(0)
            if b == KBUF:
                break
            vals_clear = by_pool(pool.memset(vals[b % KBUF][:, :, :, :], 0.0))
            wait(pool, vals_clear)
            for m in range(2):
                pool_from(BLK * m)
                vals_ok = by_pool(pool.memset(vals[b % KBUF][BLK * m:BLK * (m + 1), :, :, 16 * m + D:16 * m + D + 1], 1.0))
        h2_zero = by_dve(dve.memset(h2[:, 0:1], 0.0))

        slot_free = [(), ()]
        turn = [0]

        def slot():
            n = turn[0] % 2
            turn[0] += 1
            wait(pe, *slot_free[n])
            return n, ps_work[:, n, :, :]

        wait(act, small)
        e = by_act(act.activation(c_tmp[:, 0, :], c_sb[:, :], ACT.Exp, scale=-1.0))
        wait(dve, e)
        e = by_dve(dve.tensor_scalar(c_tmp[:, 1, :], c_tmp[:, 0, :], 1.0, None, ALU.add))
        wait(dve, e)
        e = by_dve(dve.reciprocal(c_tmp[:, 2, :], c_tmp[:, 1, :]))
        wait(dve, e, small)
        silu_ok = by_dve(dve.tensor_tensor(c_tmp[:, 0, :], c_tmp[:, 2, :], c_sb[:, :], ALU.mult))
        n, ps = slot()
        wait(pe, silu_ok, identF_ok)
        e = by_pe(pe.transpose(ps[:, 0, 0:B], c_tmp[:, 0, :], identF[0:B, 0:B]))
        wait(dve, e)
        siluT_ok = by_dve(dve.tensor_copy(siluT[:, :], ps[:, 0, 0:B]))
        slot_free[n] = (siluT_ok,)
        wait(dve, siluT_ok)
        wide_ok = by_dve(dve.tensor_copy(silu_wide[:, :, :], siluT[:, :].unsqueeze(2).to_broadcast([P, B, P])))
        n, ps = slot()
        wait(pe, siluT_ok, weights)
        for k, j in enumerate((0, 1, 3, 4)):
            e = by_pe(pe.matmul(ps[:, 0, k * B:(k + 1) * B], wmod_sb[:, j * E:(j + 1) * E], siluT[:, :],
                                start=True, stop=True))
        mod_ps = ps[:, 0, 0:4 * B].rearrange("p (k b) -> p k b", k=4)
        wait(dve, e)
        by_dve(dve.tensor_copy(modT[:, 0::2, :], mod_ps[:, 0::2, :]))
        modT_ok = by_dve(dve.tensor_scalar(modT[:, 1::2, :], mod_ps[:, 1::2, :], 1.0, None, ALU.add))
        slot_free[n] = (modT_ok,)
        wait(dve, weights)
        for k in range(2):
            for m in range(2):
                wqk_ok = by_dve(dve.tensor_copy(
                    wqk[:, k, BLK * m:BLK * (m + 1)].rearrange("c (d p) -> c d p", d=D),
                    w_in[:, k, :].rearrange("c (p m d) -> c m d p", m=2, d=D)[:, m, :, :]))
        wait(dve, small)
        wqk_ok = by_dve(dve.tensor_scalar(bq_scaled[:, :], cols[:, 0:1], D ** -0.5, None, ALU.mult))

        def gates_and_gated_weights():
            n, ps = slot()
            wait(pe, wide_ok)
            for b in range(B):
                e = by_pe(pe.matmul(ps[:, b // 2, (b % 2) * 2 * E:(b % 2 + 1) * 2 * E],
                                    silu_wide[:, b, :],
                                    wmod_sb[:, :].rearrange("p (k e) -> p k e", k=6)[:, 2::3, :], start=True, stop=True))
            raw = ps[:, :, :].rearrange("p a f -> p (a f)")
            wait(dve, e)
            gate_sign, gate_size = (probs[:, r, :, :].rearrange("p a s -> p (a s)")[:, 0:2 * B * E] for r in range(2))
            gates_flat = gates[:, :, :, :].rearrange("p b k e -> p (b k e)")
            e = by_dve(dve.tensor_scalar(gate_sign, raw, 0.0, 0.5, ALU.is_ge, ALU.subtract))
            wait(dve, e)
            e = by_dve(dve.scalar_tensor_tensor(gate_size, gate_sign, 2.0, raw, ALU.mult, ALU.mult))
            slot_free[n] = (e,)
            wait(dve, e)
            gates_ok = by_dve(dve.scalar_tensor_tensor(gates_flat, gate_size, GATE_FLOOR, gate_sign,
                                                       ALU.max, ALU.mult))
            yield
            n, ps = slot()
            wait(pe, ones_set, small, weights)
            e = by_pe(pe.matmul(ps[:, 0, 0:E], ones_row[:, :], bo_row[:, :], start=True, stop=True))
            for k in range(3):
                eT = by_pe(pe.transpose(ps[:, 1, k * E:(k + 1) * E], w_in[:, 4 + k, :], identF[:, :]))
            wait(dve, e, eT, gates_ok)
            by_dve(dve.scalar_tensor_tensor(bo_gated[:, :, :], gates[:, :, 0, :], 2.0,
                                            ps[:, 0, 0:E].unsqueeze(1).to_broadcast([P, B, E]), ALU.mult, ALU.mult))
            e = by_dve(dve.tensor_copy(wT[:, :, :], ps[:, 1, 0:3 * E].rearrange("p (k e) -> p k e", k=3)))
            slot_free[n] = (e,)
            wait(dve, e)
            by_dve(dve.scalar_tensor_tensor(wo_gated[:, :, :], gates[:, :, 0, :], 2.0,
                                            w_in[:, 3, :].unsqueeze(1).to_broadcast([P, B, E]), ALU.mult, ALU.mult))
            gated["w"] = by_dve(dve.tensor_tensor(wv_gated[:, :, :], gates[:, :, 1, :],
                                                  wT[:, 2, :].unsqueeze(1).to_broadcast([P, B, E]), ALU.mult))
            yield

        gated = {}
        last = {}

        def layer_norm(b):
            wait(dve, last.get("rstd"))
            for t in range(NT):
                e = by_dve(dve.bn_stats(stats[:, t, :], xt[:, NT * b + t, :]))
            wait(dve, e)
            for t in range(NT):
                e = by_dve(dve.bn_aggr(mean_var[:, t, :], stats[:, t, :]))
            wait(dve, e)
            e = by_dve(dve.tensor_scalar(var_eps[:, :], mean_var[:, :, 1], EPS, None, ALU.add))
            wait(pool, e, last.get("xn_made"))
            pool_from(0)
            e = by_pool(pool.tensor_tensor(rstd[:, :], var_eps[:, :], half[:, :], ALU.pow))
            last["rstd"] = e
            wait(dve, e, last.get("xn"))
            for t in range(NT):
                e = by_dve(dve.tensor_scalar(xn[:, t, :], xt[:, NT * b + t, :], mean_var[:, t, 0:1], rstd[:, t:t + 1],
                                             ALU.subtract, ALU.mult))
            last["xn_made"] = e
            return e

        def transposed(xn_ok, source):
            n, ps = slot()
            wait(pe, xn_ok)
            for t in range(NT):
                e = by_pe(pe.transpose(ps[:, 0, t * P:(t + 1) * P], source(t), identF[:, :]))
            return n, ps, e

        def prepare(b):
            wait(dve, x_in[b])
            xn_ok = layer_norm(b)
            yield
            n, ps, e = transposed(xn_ok, lambda t: xn[:, t, :])
            last["xn"] = e
            wait(act, e, modT_ok, last.get("hT"))
            hT_ok = by_act(act.activation(hT[:, :], ps[:, 0, :], ACT.Identity, bias=modT[:, 0, b:b + 1],
                                          scale=modT[:, 1, b:b + 1]))
            slot_free[n] = (hT_ok,)
            yield
            n, ps = slot()
            wait(pe, hT_ok, wqk_ok)
            for k in range(2):
                e = by_pe(pe.matmul(ps[:, k, :], wqk[:, k, :], hT[:, :], start=True, stop=True))
            wait(act, e, wqk_ok, last.get("qk32"))
            by_act(act.activation(qk32[:, 0, :], ps[:, 0, :], ACT.Identity, bias=bq_scaled[:, 0:1], scale=D ** -0.5))
            qk_ok = by_act(act.activation(qk32[:, 1, :], ps[:, 1, :], ACT.Identity, bias=cols[:, 1:2]))
            slot_free[n] = (qk_ok,)
            wait(act, qk_ok, last.get("parts_read"))
            e = by_act(act.copy(qk_parts[:, :, 0, :], qk32[:, :, :]))
            wait(pool, e)
            pool_from(0)
            e = by_pool(pool.tensor_tensor(qk_rest[:, :, :], qk32[:, :, :], qk_parts[:, :, 0, :], ALU.subtract))
            last["qk32"] = e
            yield
            n, ps = slot()
            for i in range(NB):
                for m in range(2):
                    eV = by_pe(pe.matmul(ps[BLK * m:BLK * (m + 1), 0, BLK * i:BLK * (i + 1)],
                                         hT[:, BLK * i:BLK * (i + 1)],
                                         w_in[:, 2, :].rearrange("c (p m d) -> c m p d", m=2, d=D)[:, m, :, :],
                                         start=True, stop=True))
            last["hT"] = eV
            wait(act, eV, vals_ok, last.get(("vals", b % KBUF)))
            wait(dve, eV, vals_ok, last.get(("vals", b % KBUF)))
            for m, eng in ((0, act), (1, dve)):
                dst = vals[b % KBUF][BLK * m:BLK * (m + 1), :, :, 16 * m:16 * m + D]
                src = ps[BLK * m:BLK * (m + 1), 0, :].rearrange("p (i h d) -> p i h d", i=NB, d=D)
                if m == 0:
                    v0 = by_act(act.copy(dst, src))
                else:
                    v1 = by_dve(dve.tensor_copy(dst, src))
            wait(dve, v0)
            slot_free[n] = (v0, v1)
            vals_in[b] = (v0, v1)
            wait(act, e)
            e = by_act(act.copy(qk_parts[:, :, 1, :], qk_rest[:, :, :]))
            wait(pool, e)
            pool_from(0)
            e = by_pool(pool.tensor_tensor(qk_parts[:, :, 2, :], qk_rest[:, :, :], qk_parts[:, :, 1, :], ALU.subtract))
            wait(sp, e, q_clear[b], k_clear[b % KBUF], last.get(("k_ops", b % KBUF)))
            for r, (qp, kp) in enumerate(PRODUCTS):
                for m in range(2):
                    h, rows = slice(BLK * m, BLK * (m + 1)), slice(BLK * m + D * r, BLK * m + D * (r + 1))
                    done(sp.dma_start(q_ops[b][rows, :, :], qk_parts[h, 0, qp, :]), s_ops[b], 16)
                    ops_in[b] = done(sp.dma_start(k_ops[b % KBUF][rows, m, :, :], qk_parts[h, 1, kp, :]), s_ops[b], 16)
            last["parts_read"] = ops_in[b]
            wait(pool, xn_ok, gated["w"])
            xb = xt[:, NT * b:NT * (b + 1), :]
            pool_from(0)
            x_biased[b] = by_pool(pool.tensor_tensor(xb, xb, bo_gated[:, b, :].unsqueeze(1).to_broadcast([P, NT, E]),
                                                     ALU.add))
            yield

        vals_in, ops_in, x_biased, maxima_in = {}, {}, {}, {}

        def window(i):
            lo, hi = max(i - REACH, 0), min(i + REACH + 1, NB)
            return lo, hi, BLK * (lo - i + REACH), BLK * (hi - i + REACH)

        def max_scores(n, u):
            b, g = divmod(n, NG)
            pp, i2 = divmod(u, NB // 2)
            pair = GP * g + pp
            i = 2 * i2
            w0 = REACH - i - 1 if i < REACH else 0
            w1 = NB - i + REACH - 1 if i + 1 >= NB - REACH else WIN - 1
            b0 = 0 if i < REACH else 1
            b1 = 3 if i + 1 >= NB - REACH else 2
            k, ps = slot()
            wait(pe, ops_in[b], band_ok, identB_ok)
            for m in range(2):
                wide = ps[:, m, 0:WIN * BLK].rearrange("p (w s) -> p w s", w=WIN)
                by_pe(pe.matmul(wide[:, w0:w1 + 1:w1 - w0, :], identB[:, :], band[:, b0:b1 + 1:b1 - b0, :],
                                start=True, stop=False, skip_group_check=True))
            for m in range(2):
                for j in range(2):
                    lo, hi, c0, c1 = window(i + j)
                    e = by_pe(pe.matmul(ps[BLK * j:BLK * (j + 1), m, c0:c1], q_ops[b][:, pair, BLK * (i + j):BLK * (i + j + 1)],
                                        k_ops[b % KBUF][:, m, pair, BLK * lo:BLK * hi], start=False, stop=True,
                                        skip_group_check=True))
            wait(dve, e, last.get(("neg_max", n % 2)))
            e = by_dve(dve.tensor_reduce(neg_max[:, n % 2, :, pp, i2], ps[:, :, BLK * w0:BLK * (w1 + 1)], AX.X, ALU.max,
                                         negate=True))
            slot_free[k] = (e,)
            return e

        def place_maxima(n, e):
            b, g = divmod(n, NG)
            nm = neg_max[:, n % 2, :, :, :].rearrange("p m a i -> p m (a i)")
            wait(dve, e, last.get("max_parts"))
            e = by_dve(dve.tensor_copy(max_parts[:, :, 0, :], nm))
            wait(dve, e)
            e = by_dve(dve.tensor_tensor(max_rest[:, :, :], nm, max_parts[:, :, 0, :], ALU.subtract))
            last[("neg_max", n % 2)] = e
            wait(dve, e)
            e = by_dve(dve.tensor_copy(max_parts[:, :, 1, :], max_rest[:, :, :]))
            wait(dve, e)
            e = by_dve(dve.tensor_tensor(max_parts[:, :, 2, :], max_rest[:, :, :], max_parts[:, :, 1, :], ALU.subtract))
            yield
            k, ps = slot()
            wait(pe, e)
            psb = ps[0:PARTS * GP * NB, 0, 0:P // 2].bitcast(BF16)
            e = by_pe(pe.transpose(psb, max_parts[:, :, :, :].rearrange("p m a i -> p (m a i)"), identB[:, :]))
            last["max_parts"] = e
            wait(act, e, maxima_in.get(n - 2))
            e = by_act(act.copy(max_rows[:, n % 2, :], psb))
            slot_free[k] = (e,)
            wait(sp, e)
            for m in range(2):
                r, h = BLK * m + ROWS, PARTS * GP * NB // 2
                maxima_in[n] = done(sp.dma_start(q_ops[b][r:r + PARTS, GP * g:GP * (g + 1), :],
                                                 max_rows[h * m:h * (m + 1), n % 2, :]), s_max[n], 16)
            yield

        exp_free = [None] * 3
        exp_turn = [0]
        probs_free = {}
        probs_in = {}

        def exp_scores(s, pp):
            n, i = divmod(s, NB)
            b, g = divmod(n, NG)
            pair = GP * g + pp
            lo, hi, c0, c1 = window(i)
            k = exp_turn[0] % 3
            exp_turn[0] += 1
            wait(pe, maxima_in[n], exp_free[k])
            for m in range(2):
                e = by_pe(pe.matmul(ps_exp[BLK * m:BLK * (m + 1), k, c0:c1],
                                    k_ops[b % KBUF][:, m, pair, BLK * i:BLK * (i + 1)],
                                    q_ops[b][:, pair, BLK * lo:BLK * hi], start=True, stop=True))
            last[("k_ops", b % KBUF)] = e
            wait(act, e, probs_free.get(s - RING))
            exp_free[k] = by_act(act.activation(probs[:, s % RING, pp, c0:c1], ps_exp[:, k, c0:c1], ACT.Exp))
            return exp_free[k]

        def mask_probs(s, e):
            i = s % NB
            wait(pool, e)
            for w, sign in ((0, 1), (WIN - 1, -1)):
                if not (i >= REACH if w == 0 else i < NB - REACH):
                    continue
                for m in range(2):
                    t = probs[BLK * m:BLK * (m + 1), s % RING, :, w * BLK:(w + 1) * BLK]
                    pool_from(BLK * m)
                    e = by_pool(pool.affine_select(out=t, in_=t, compare_op=ALU.is_ge, fill=0.0, base=0,
                                                   pattern=[[0, GP], [sign, BLK]], channel_multiplier=-sign))
            probs_in[s] = e

        def weighted_sums(s):
            n, i = divmod(s, NB)
            b, g = divmod(n, NG)
            lo, hi, c0, c1 = window(i)
            wait(pe, probs_in[s], *vals_in[b])
            if i == 0:
                wait(pe, last.get("ps_sum"))
            for pp in range(GP):
                e = by_pe(pe.matmul(ps_sum[VW * pp:VW * (pp + 1), BLK * lo:BLK * hi], vals[b % KBUF][:, i, GP * g + pp, :],
                                    probs[:, s % RING, pp, c0:c1], start=(i == 0), stop=(i == NB - 1),
                                    skip_group_check=True))
            probs_free[s] = last[("vals", b % KBUF)] = e
            if i == NB - 1:
                wait(act, e, last.get(("sums_T", n % 2)))
                last["ps_sum"] = by_act(act.copy(sums_T[:, n % 2, :], ps_sum[:, :]))
                return last["ps_sum"]

        def normalise(n, e):
            b, g = divmod(n, NG)
            k, ps, e = transposed(e, lambda t: sums_T[:, n % 2, t * P:(t + 1) * P])
            last[("sums_T", n % 2)] = e
            sums = ps[:, 0, :].rearrange("p (t h w) -> p t h w", t=NT, w=16)
            wait(dve, e, last.get("o_tok") if g == 0 else None)
            e = by_dve(dve.reciprocal(inv[:, n % 2, :, :], sums[:, :, :, D]))
            wait(dve, e)
            dst = o_tok[:, :, :].rearrange("p t (g h d) -> p t g h d", g=NG, d=D)[:, :, g, :, :]
            e = by_dve(dve.tensor_tensor(dst, sums[:, :, :, 0:D],
                                         inv[:, n % 2, :, :].unsqueeze(3).to_broadcast([P, NT, 2 * GP, D]), ALU.mult))
            slot_free[k] = (e,)
            normalised[n] = e
            yield

        normalised = {}

        def finish(b):
            xb = xt[:, NT * b:NT * (b + 1), :]
            n, ps, e = transposed(normalised[NG * b + NG - 1], lambda t: o_tok[:, t, :])
            last["o_tok"] = e
            wait(act, e, last.get("o_T"), small)
            e = by_act(act.activation(o_T[:, :], ps[:, 0, :], ACT.Identity, bias=cols[:, 2:3]))
            slot_free[n] = (e,)
            yield
            n, ps = slot()
            wait(pe, e, gated["w"])
            for t in range(NT):
                e = by_pe(pe.matmul(ps[:, 0, t * P:(t + 1) * P], o_T[:, t * P:(t + 1) * P], wo_gated[:, b, :],
                                    start=True, stop=True))
            last["o_T"] = e
            wait(dve, e, x_biased[b])
            e = by_dve(dve.tensor_tensor(xb, ps[:, 0, :].rearrange("p (t e) -> p t e", t=NT), xb, ALU.add))
            slot_free[n] = (e,)
            wait(dve, e)
            x1_ok = e
            xn_ok = layer_norm(b)
            yield
            n, ps, e = transposed(xn_ok, lambda t: xn[:, t, :])
            last["xn"] = e
            wait(act, e, h2_zero, last.get("h2"))
            h2_ok = by_act(act.activation(h2[:, 1:1 + S], ps[:, 0, :], ACT.Identity, bias=modT[:, 2, b:b + 1],
                                          scale=modT[:, 3, b:b + 1]))
            slot_free[n] = (h2_ok,)
            wait(pool, h2_ok, last.get("h2_diff"))
            pool_from(0)
            e = by_pool(pool.tensor_tensor(h2_diff[:, :], h2[:, 1:1 + S], h2[:, 0:S], ALU.subtract))
            yield
            wait(dve, e, small, last.get("mixed"))
            for k in range(2):
                mix_ok = by_dve(dve.scalar_tensor_tensor(mixed[:, k, :], h2_diff[:, :], cols[:, 3 + k:4 + k], h2[:, 0:S],
                                                         ALU.mult, ALU.add))
            last["h2"] = last["h2_diff"] = mix_ok
            yield
            n, ps = slot()
            wait(pe, mix_ok, gated["w"])
            for t in range(NT):
                by_pe(pe.matmul(ps[:, 0, t * P:(t + 1) * P], mixed[:, 0, t * P:(t + 1) * P], wT[:, 0, :],
                                start=True, stop=True))
            e = by_pe(pe.matmul(ps[:, 1, :], wT[:, 1, :], mixed[:, 1, :], start=True, stop=True))
            last["mixed"] = e
            wait(act, e, last.get("gate_r"), last.get("k_relu"))
            by_act(act.activation(gate_r[:, :, :].rearrange("p t e -> p (t e)"), ps[:, 0, :], ACT.Tanh, scale=0.5))
            e = by_act(act.activation(k_relu[:, :], ps[:, 1, :], ACT.Relu))
            slot_free[n] = (e,)
            wait(pool, e, last.get("k_sq"))
            pool_from(0)
            ksq_ok = by_pool(pool.tensor_tensor(k_sq[:, :], k_relu[:, :], k_relu[:, :], ALU.mult))
            last["k_relu"] = ksq_ok
            yield
            n, ps = slot()
            wait(pe, ksq_ok)
            for t in range(NT):
                e = by_pe(pe.matmul(ps[:, 0, t * P:(t + 1) * P], k_sq[:, t * P:(t + 1) * P], wv_gated[:, b, :],
                                    start=True, stop=True))
            last["k_sq"] = e
            wait(dve, e, last.get("y2"))
            e = by_dve(dve.scalar_tensor_tensor(y2[:, :, :].rearrange("p t e -> p (t e)"),
                                                gate_r[:, :, :].rearrange("p t e -> p (t e)"), 1.0, ps[:, 0, :],
                                                ALU.add, ALU.mult))
            slot_free[n] = (e,)
            last["gate_r"] = e
            wait(pool, e, x1_ok)
            pool_from(0)
            e = by_pool(pool.tensor_tensor(xb, xb, y2[:, :, :], ALU.add))
            last["y2"] = e
            wait(sp, e)
            stored[0] = done(sp.dma_start(out[b].rearrange("(t p) e -> p t e", p=P), xb), s_out, 16)
            yield

        stored = [None]

        def run(steps):
            for _ in steps:
                pass

        LEAD = 4
        UNITS = GP * NB // 2
        NGROUPS = B * NG
        tasks = []
        run(gates_and_gated_weights())
        run(prepare(0))
        max_done = {}

        def max_step(q):
            n, u = divmod(q, UNITS)
            if n >= NGROUPS:
                return
            e = max_scores(n, u)
            if u == UNITS - 1:
                placing.append(place_maxima(n, e))

        placing = []
        for q in range(UNITS):
            max_step(q)
        run(placing.pop(0))
        tasks.append(prepare(1))
        for q in range(UNITS, UNITS + 2 * LEAD):
            max_step(q)
        finished = []
        for s in range(STEPS + 1):
            n, i = divmod(s, NB)
            q = UNITS + 2 * (s + LEAD)
            e = None
            for pp in range(GP):
                if s < STEPS:
                    e = exp_scores(s, pp)
                if pp % 2 == 1:
                    max_step(q + pp // 2)
            if s < STEPS:
                mask_probs(s, e)
            if placing:
                if next(placing[0], "end") == "end":
                    placing.pop(0)
            if s >= 1:
                e = weighted_sums(s - 1)
                if e is not None:
                    m = (s - 1) // NB
                    finished.append((m, e))
            if finished and (i == 2 or s == STEPS):
                m, e = finished.pop(0)
                run(normalise(m, e))
                if m % NG == NG - 1:
                    tasks.append(finish(m // NG))
            if s % (NG * NB) == NB - 2 and s // (NG * NB) + 2 < B:
                tasks.append(prepare(s // (NG * NB) + 2))
            if tasks:
                if next(tasks[0], "end") == "end":
                    tasks.pop(0)
        for t in tasks:
            run(t)
        wait(sp, stored[0])


_INS = ['L0_attn_x', 'L0_attn_Wq', 'L0_attn_bq', 'L0_attn_Wk', 'L0_attn_bk', 'L0_attn_Wv', 'L0_attn_bv',
        'L0_attn_Wo', 'L0_attn_bo', 'L0_ffn_W_r', 'L0_ffn_W_k', 'L0_ffn_W_v', 'L0_ffn_mu_r', 'L0_ffn_mu_k',
        'L0_c', 'L0_wmod']


def kernel(**inputs):
    import numpy as _np
    import concourse.bacc as _bacc
    from concourse import mybir as _mybir
    from concourse.bass_utils import run_bass_kernel_spmd as _run

    nc = _bacc.Bacc("TRN2", target_bir_lowering=False, num_devices=1)
    arrays, args = {}, []
    for name in _INS:
        a = _np.ascontiguousarray(inputs[name])
        arrays[f"in_{name}_dram"] = a
        args.append(nc.dram_tensor(f"in_{name}_dram", a.shape, _mybir.dt.from_np(a.dtype), kind="ExternalInput").ap())
    shape = inputs['L0_attn_x'].shape
    args.append(nc.dram_tensor("out_0_dram", shape, _mybir.dt.float32, kind="ExternalOutput").ap())
    adaln_block(nc, *args)
    r = _run(nc, [arrays], core_ids=[0])
    return r.results[0]["out_0_dram"]
```

```python
from contextlib import ExitStack

import numpy as np

import concourse.bass as bass
from concourse import mybir

F32 = mybir.dt.float32
BF16 = mybir.dt.bfloat16
ACT = mybir.ActivationFunctionType
ALU = mybir.AluOpType
AX = mybir.AxisListType

P = 128
EPS = 1e-5
GATE_FLOOR = 0.25
MASKED = -1e30
ONES = float(np.array([0x3F803F80], np.uint32).view(np.float32)[0])


def adaln_block(nc, x, Wq, bq, Wk, bk, Wv, bv, Wo, bo, W_r, W_k, W_v, mu_r, mu_k, c, wmod, out):
    B, S, E = x.shape
    D = 8
    NT = S // P
    BLK = 64
    NB = S // BLK
    REACH = P // BLK
    WIN = 2 * REACH + 1
    PAIRS = E // D // 2
    GP = 4
    NG = PAIRS // GP
    STEPS = B * NG * NB
    PARTS = 3
    PRODUCTS = [(0, 0), (0, 1), (1, 0), (1, 1), (0, 2), (2, 0)]
    ROWS = len(PRODUCTS) * 2 * D
    MAX_ROWS = 2 * PARTS
    POOL_PAIRS = 3
    KBUF = 3
    VW = 32
    assert E == P and S % P == 0 and NG * GP == PAIRS and GP * VW == P

    ctx = ExitStack()
    with ctx:
        def sb(name, shape, dt=F32):
            return ctx.enter_context(nc.sbuf_tensor(name, shape, dt))

        def sem(name):
            return ctx.enter_context(nc.semaphore(name))

        pe, dve, act, pool, sp = nc.tensor, nc.vector, nc.scalar, nc.gpsimd, nc.sync

        s_pe, s_dve, s_act, s_pool = sem("s_pe"), sem("s_dve"), sem("s_act"), sem("s_pool")
        count, seen = {}, {}

        def done(instruction, semaphore, by=1):
            instruction.then_inc(semaphore, by)
            count[id(semaphore)] = count.get(id(semaphore), 0) + by
            return semaphore, count[id(semaphore)]

        def wait(engine, *events):
            for event in events:
                if event is None:
                    continue
                semaphore, value = event
                key = (id(engine), id(semaphore))
                if seen.get(key, 0) < value:
                    engine.wait_ge(semaphore, value)
                    seen[key] = value

        def by_pe(i):
            return done(i, s_pe)

        def by_dve(i):
            return done(i, s_dve)

        def by_act(i):
            return done(i, s_act)

        def by_pool(i):
            return done(i, s_pool)

        pool_start = [0]

        def pool_from(partition):
            if pool_start[0] != partition:
                wait(pool, (s_pool, count[id(s_pool)]))
                pool_start[0] = partition

        xt = sb("xt", [P, B * NT, E])
        w_in = sb("w_in", [P, 7, E])
        wqk = sb("wqk", [P, 2, E])
        wT = sb("wT", [P, 3, E])
        wo_gated = sb("wo_gated", [P, B, E])
        wv_gated = sb("wv_gated", [P, B, E])
        wmod_sb = sb("wmod_sb", [P, 6 * E])
        cols = sb("cols", [P, 5])
        bq_scaled = sb("bq_scaled", [P, 1])
        bo_row = sb("bo_row", [1, E])
        ones_row = sb("ones_row", [1, P])
        c_sb = sb("c_sb", [B, E])
        c_tmp = sb("c_tmp", [B, 3, E])
        siluT = sb("siluT", [P, B])
        silu_wide = sb("silu_wide", [P, B, P])
        modT = sb("modT", [P, 4, B])
        gates = sb("gates", [P, B, 2, E])
        bo_gated = sb("bo_gated", [P, B, E])
        identF = sb("identF", [P, P])
        identB = sb("identB", [P, P], BF16)
        band = sb("band", [P, 4, BLK], BF16)
        half = sb("half", [P, NT])
        warm = sb("warm", [P, 1])

        stats = sb("stats", [P, NT, 6])
        mean_var = sb("mean_var", [P, NT, 2])
        var_eps = sb("var_eps", [P, NT])
        rstd = sb("rstd", [P, NT])
        mean_rstd = sb("mean_rstd", [P, NT])
        neg_mean_rstd = sb("neg_mean_rstd", [P, NT])
        xn = sb("xn", [P, NT, E])
        hT = sb("hT", [P, S])
        qk32 = sb("qk32", [P, 2, S])
        qk_rest = sb("qk_rest", [P, 2, S])
        qk_parts = sb("qk_parts", [P, 2, PARTS, S], BF16)
        q_ops = [sb(f"q_ops{b}", [P, PAIRS, S], BF16) for b in range(B)]
        k_ops = [sb(f"k_ops{b}", [P, 2, PAIRS, S], BF16) for b in range(KBUF)]
        vals = [sb(f"vals{b}", [P, NB, PAIRS, VW]) for b in range(KBUF)]
        neg_max = sb("neg_max", [P, 2, 2, GP, NB // 2])
        max_rest = sb("max_rest", [P, 2, GP * NB // 2])
        max_parts = sb("max_parts", [P, 2, PARTS, GP * NB // 2], BF16)
        max_ones = sb("max_ones", [MAX_ROWS, 2, S], BF16)
        max_rows = sb("max_rows", [2 * PARTS * GP * NB // 2, 2, P], BF16)
        RING = 4
        probs = sb("probs", [P, RING, GP, WIN * BLK])
        sums_T = sb("sums_T", [P, 2, S])
        inv = sb("inv", [P, 2, NT, 2 * GP])
        o_tok = sb("o_tok", [P, NT, E])
        o_T = sb("o_T", [P, S])
        h2 = sb("h2", [P, 1 + S])
        h2_diff = sb("h2_diff", [P, S])
        mixed = sb("mixed", [P, 2, S])
        gate_r = sb("gate_r", [P, NT, E])
        k_relu = sb("k_relu", [P, S])
        k_sq = sb("k_sq", [P, S])
        y2 = sb("y2", [P, NT, E])

        ps_work = ctx.enter_context(nc.psum_tensor("ps_work", [P, 2, 2, 512], F32))
        ps_exp = ctx.enter_context(nc.psum_tensor("ps_exp", [P, 3, 512], F32))
        ps_sum = ctx.enter_context(nc.psum_tensor("ps_sum", [P, 512], F32))

        s_x = [sem(f"s_x{b}") for b in range(B)]
        s_c, s_wmod, s_qkv, s_mix, s_small, s_out = (sem(n) for n in ("s_c", "s_wmod", "s_qkv", "s_mix", "s_small", "s_out"))
        s_q = [sem(f"s_q{b}") for b in range(B)]
        s_k = [sem(f"s_k{b}") for b in range(B)]
        s_k_second = sem("s_k_second")
        s_ones = [sem(f"s_ones{b}") for b in range(KBUF)]
        s_max = [sem(f"s_max{n}") for n in range(B * NG)]

        def load_x(b):
            return done(sp.dma_start(xt[:, NT * b:NT * (b + 1), :], x[b].rearrange("(t p) e -> p t e", p=P)), s_x[b], 16)

        c_in = done(act.dma_start(c_sb[:, :], c), s_c, 16)
        x_in = {0: load_x(0)}
        wmod_in = done(act.dma_start(wmod_sb[:, :], wmod), s_wmod, 16)
        for n, w in enumerate((Wq, Wk, Wv)):
            qkv_in = done(sp.dma_start(w_in[:, n, :], w), s_qkv, 16)
        with nc.allow_non_contiguous_dma(reason="bias columns, 128 elements each"):
            for n, v in enumerate((bq, bk)):
                for m in range(2):
                    small = done(act.dma_start(cols[BLK * m:BLK * (m + 1), n:n + 1],
                                               v.rearrange("(p m d) -> m d p", m=2, d=D)[m]), s_small, 16)
            for n, v in enumerate((bv, mu_r, mu_k)):
                small = done(sp.dma_start(cols[:, 2 + n:3 + n], v.rearrange("(p a) -> p a", a=1)), s_small, 16)
        small = done(sp.dma_start(bo_row[:, :], bo.rearrange("(a d) -> a d", a=1)), s_small, 16)
        for b in range(1, B):
            x_in[b] = load_x(b)
            if b == 1:
                for n, w in enumerate((Wo, W_r, W_k, W_v)):
                    mix_in = done(sp.dma_start(w_in[:, 3 + n, :], w), s_mix, 16)

        q_clear, k_clear, vals_ok, ones_in = {}, {}, {}, {}

        def words(t):
            return t.rearrange("p a s -> p (a s)").bitcast(F32)

        def clear_q(b):
            q_clear[b] = by_pool(pool.memset(words(q_ops[b][:, :, :]), 0.0))

        def clear_k(b):
            for m in range(2):
                k_clear[b] = by_pool(pool.memset(words(k_ops[b][:, m, :, :]), 0.0))

        def load_ones(b):
            wait(sp, k_clear[b], max_ones_ok)
            for m in range(2):
                ones_in[b] = done(sp.dma_start(k_ops[b][ROWS:ROWS + MAX_ROWS, m, :, :],
                                               max_ones[:, m, :].unsqueeze(1).to_broadcast([MAX_ROWS, PAIRS, S])),
                                  s_ones[b], 16)

        def clear_vals(b):
            pool_from(0)
            e = by_pool(pool.memset(vals[b][:, :, :, :], 0.0))
            wait(pool, e)
            for m in range(2):
                pool_from(BLK * m)
                vals_ok[b] = by_pool(pool.memset(vals[b][BLK * m:BLK * (m + 1), :, :, 16 * m + D:16 * m + D + 1], 1.0))

        half_ok = by_pool(pool.memset(half[:, :], -0.5))
        by_pool(pool.memset(identF[:, :], 0.0))
        max_ones_set = by_pool(pool.memset(max_ones[:, :, :], 1.0))
        zeroed = by_pool(pool.memset(band[:, :, :], 0.0))
        wait(pool, zeroed)
        pool_from(0)
        identF_ok = by_pool(pool.affine_select(out=identF[:, :], in_=identF[:, :], compare_op=ALU.not_equal, fill=1.0,
                                               base=0, pattern=[[-1, P]], channel_multiplier=1))
        clear_q(0)
        clear_k(0)
        for m in range(2):
            rows = slice(BLK * m, BLK * (m + 1))
            pool_from(BLK * m)
            by_pool(pool.affine_select(out=band[rows, 1, :], in_=band[rows, 1, :], compare_op=ALU.is_ge, fill=MASKED,
                                       base=0, pattern=[[1, BLK]], channel_multiplier=-1))
            by_pool(pool.affine_select(out=band[rows, 2, :], in_=band[rows, 2, :], compare_op=ALU.is_ge,
                                       fill=MASKED, base=0, pattern=[[-1, BLK]], channel_multiplier=1))
            band_ok = by_pool(pool.memset(band[rows, 3 * m, :], MASKED))
        pool_from(0)
        wait(pool, max_ones_set)
        for m in range(2):
            sign = 1 if m else -1
            max_ones_ok = by_pool(pool.affine_select(
                out=max_ones[:, m, :], in_=max_ones[:, m, :], compare_op=ALU.is_ge, fill=0.0,
                base=-PARTS if m else PARTS - 1, pattern=[[0, S]], channel_multiplier=sign))
        load_ones(0)
        clear_vals(0)
        wait(act, half_ok)
        by_act(act.activation(warm[:, :], half[:, 0:1], ACT.Exp))

        ones_set = by_dve(dve.memset(ones_row[:, :], 1.0))
        h2_zero = by_dve(dve.memset(h2[:, 0:1], 0.0))
        wait(dve, identF_ok)
        identB_ok = by_dve(dve.tensor_copy(identB[:, :], identF[:, :]))

        bank_free = [()] * 3
        bank_turn = [0]

        def bank():
            n = bank_turn[0] % 3
            bank_turn[0] += 1
            wait(pe, *bank_free[n])
            return n, ps_exp[:, n, :]

        slot_free = [(), ()]
        turn = [0]

        def slot():
            n = turn[0] % 2
            turn[0] += 1
            wait(pe, *slot_free[n])
            return n, ps_work[:, n, :, :]

        def gates_and_gated_weights():
            n, ps = slot()
            wait(pe, wide_ok)
            for b in range(B):
                e = by_pe(pe.matmul(ps[:, b // 2, (b % 2) * 2 * E:(b % 2 + 1) * 2 * E],
                                    silu_wide[:, b, :],
                                    wmod_sb[:, :].rearrange("p (k e) -> p k e", k=6)[:, 2::3, :], start=True, stop=True))
            raw = ps[:, :, :].rearrange("p a f -> p (a f)")
            wait(dve, e)
            gate_sign, gate_size = (t[:, :, :].rearrange("p k s -> p (k s)") for t in (mixed, sums_T))
            gates_flat = gates[:, :, :, :].rearrange("p b k e -> p (b k e)")
            e = by_dve(dve.tensor_scalar(gate_sign, raw, 0.0, 0.5, ALU.is_ge, ALU.subtract))
            wait(dve, e)
            e = by_dve(dve.scalar_tensor_tensor(gate_size, gate_sign, 2.0, raw, ALU.mult, ALU.mult))
            slot_free[n] = (e,)
            wait(dve, e)
            gates_ok = by_dve(dve.scalar_tensor_tensor(gates_flat, gate_size, GATE_FLOOR, gate_sign,
                                                       ALU.max, ALU.mult))
            last["mixed"] = last["sums_T", 0] = last["sums_T", 1] = gates_ok
            yield
            n, ps = slot()
            wait(pe, ones_set, small, mix_in)
            e = by_pe(pe.matmul(ps[:, 0, 0:E], ones_row[:, :], bo_row[:, :], start=True, stop=True))
            for k in range(3):
                eT = by_pe(pe.transpose(ps[:, 1, k * E:(k + 1) * E], w_in[:, 4 + k, :], identF[:, :]))
            wait(dve, e, eT, gates_ok, mix_in)
            by_dve(dve.scalar_tensor_tensor(bo_gated[:, :, :], gates[:, :, 0, :], 2.0,
                                            ps[:, 0, 0:E].unsqueeze(1).to_broadcast([P, B, E]), ALU.mult, ALU.mult))
            e = by_dve(dve.tensor_copy(wT[:, :, :], ps[:, 1, 0:3 * E].rearrange("p (k e) -> p k e", k=3)))
            slot_free[n] = (e,)
            wait(dve, e)
            by_dve(dve.scalar_tensor_tensor(wo_gated[:, :, :], gates[:, :, 0, :], 2.0,
                                            w_in[:, 3, :].unsqueeze(1).to_broadcast([P, B, E]), ALU.mult, ALU.mult))
            gated["w"] = by_dve(dve.tensor_tensor(wv_gated[:, :, :], gates[:, :, 1, :],
                                                  wT[:, 2, :].unsqueeze(1).to_broadcast([P, B, E]), ALU.mult))
            yield

        gated = {}
        last = {}

        xn_ok = {}

        def layer_norm(b, hurried=False):
            wait(dve, last.get("rstd"), last.get("xn_made"))
            for t in range(NT):
                e = by_dve(dve.bn_stats(stats[:, t, :], xt[:, NT * b + t, :]))
            wait(dve, e)
            for t in range(NT):
                e = by_dve(dve.bn_aggr(mean_var[:, t, :], stats[:, t, :]))
            wait(dve, e)
            e = by_dve(dve.tensor_scalar(var_eps[:, :], mean_var[:, :, 1], EPS, None, ALU.add))
            wait(pool, e, last.get("xn_made"))
            pool_from(0)
            e = by_pool(pool.tensor_tensor(rstd[:, :], var_eps[:, :], half[:, :], ALU.pow))
            last["rstd"] = e
            if hurried:
                wait(dve, e, last.get("xn"))
                for t in range(NT):
                    e = by_dve(dve.tensor_scalar(xn[:, t, :], xt[:, NT * b + t, :], mean_var[:, t, 0:1],
                                                 rstd[:, t:t + 1], ALU.subtract, ALU.mult))
            else:
                wait(pool, e)
                e = by_pool(pool.tensor_tensor(mean_rstd[:, :], mean_var[:, :, 0], rstd[:, :], ALU.mult))
                wait(pool, e)
                e = by_pool(pool.tensor_scalar(neg_mean_rstd[:, :], mean_rstd[:, :], -1.0, None, ALU.mult))
                yield
                yield
                wait(act, e, last.get("xn"))
                for t in range(NT):
                    e = by_act(act.activation(xn[:, t, :], xt[:, NT * b + t, :], ACT.Identity, scale=rstd[:, t:t + 1],
                                              bias=neg_mean_rstd[:, t:t + 1]))
            last["xn_made"] = xn_ok[b] = e
            yield

        def transposed(ready, source):
            n, ps = bank()
            wait(pe, ready)
            for t in range(NT):
                e = by_pe(pe.transpose(ps[:, t * P:(t + 1) * P], source(t), identF[:, :]))
            return n, ps, e

        wait(dve, x_in[0])
        for _ in layer_norm(0, hurried=True):
            pass

        wait(act, c_in)
        e = by_act(act.activation(c_tmp[:, 0, :], c_sb[:, :], ACT.Exp, scale=-1.0))
        wait(dve, e)
        e = by_dve(dve.tensor_scalar(c_tmp[:, 1, :], c_tmp[:, 0, :], 1.0, None, ALU.add))
        wait(dve, e)
        e = by_dve(dve.reciprocal(c_tmp[:, 2, :], c_tmp[:, 1, :]))
        wait(dve, e, c_in)
        silu_ok = by_dve(dve.tensor_tensor(c_tmp[:, 0, :], c_tmp[:, 2, :], c_sb[:, :], ALU.mult))
        n, ps = slot()
        wait(pe, silu_ok, identF_ok)
        e = by_pe(pe.transpose(ps[:, 0, 0:B], c_tmp[:, 0, :], identF[0:B, 0:B]))
        wait(dve, e)
        siluT_ok = by_dve(dve.tensor_copy(siluT[:, :], ps[:, 0, 0:B]))
        slot_free[n] = (siluT_ok,)
        wait(dve, siluT_ok)
        wide_ok = by_dve(dve.tensor_copy(silu_wide[:, :, :], siluT[:, :].unsqueeze(2).to_broadcast([P, B, P])))
        n, ps = slot()
        wait(pe, siluT_ok, wmod_in)
        for k, j in enumerate((0, 1, 3, 4)):
            e = by_pe(pe.matmul(ps[:, 0, k * B:(k + 1) * B], wmod_sb[:, j * E:(j + 1) * E], siluT[:, :],
                                start=True, stop=True))
        mod_ps = ps[:, 0, 0:4 * B].rearrange("p (k b) -> p k b", k=4)
        wait(dve, e)
        by_dve(dve.tensor_copy(modT[:, 0::2, :], mod_ps[:, 0::2, :]))
        modT_ok = by_dve(dve.tensor_scalar(modT[:, 1::2, :], mod_ps[:, 1::2, :], 1.0, None, ALU.add))
        slot_free[n] = (modT_ok,)
        wait(dve, qkv_in)
        for k in range(2):
            for m in range(2):
                wqk_ok = by_dve(dve.tensor_copy(
                    wqk[:, k, BLK * m:BLK * (m + 1)].rearrange("c (d p) -> c d p", d=D),
                    w_in[:, k, :].rearrange("c (p m d) -> c m d p", m=2, d=D)[:, m, :, :]))
        wait(dve, small)
        wqk_ok = by_dve(dve.tensor_scalar(bq_scaled[:, :], cols[:, 0:1], D ** -0.5, None, ALU.mult))

        def prepare(b):
            if b:
                wait(dve, x_in[b])
                yield from layer_norm(b)
            n, ps, e = transposed(xn_ok[b], lambda t: xn[:, t, :])
            last["xn"] = e
            wait(act, e, modT_ok, last.get("hT"))
            hT_ok = by_act(act.activation(hT[:, :], ps, ACT.Identity, bias=modT[:, 0, b:b + 1],
                                          scale=modT[:, 1, b:b + 1]))
            bank_free[n] = (hT_ok,)
            yield
            sub, by_sub = (dve, by_dve) if b == 0 else (pool, by_pool)

            def subtract(rest, value, part):
                if b:
                    pool_from(0)
                return by_sub(sub.tensor_tensor(rest, value, part, ALU.subtract))

            def load_parts(k, part, ready):
                rows = [2 * D * r for r, product in enumerate(PRODUCTS) if product[k] == part]
                if k == 0:
                    wait(sp, ready, q_clear[b])
                    for r in rows:
                        ops_in[b, 0] = done(sp.dma_start(q_ops[b][r:r + 2 * D, :, :], qk_parts[:, 0, part, :]), s_q[b], 16)
                    return
                for m in range(2):
                    second = b == 0 and m == 1
                    engine = pool if second else sp
                    wait(engine, ready, k_clear[b % KBUF], last.get(("k_ops", b % KBUF)))
                    for r in rows:
                        ops_in[b, 2 if second else 1] = done(
                            engine.dma_start(k_ops[b % KBUF][r + D * m:r + D * (m + 1), m, :, :],
                                             qk_parts[BLK * m:BLK * (m + 1), 1, part, :]),
                            s_k_second if second else s_k[b], 16)

            rest_ok = [None, None]
            for k in range(2):
                n, ps = bank()
                wait(pe, hT_ok, wqk_ok, qkv_in)
                e = by_pe(pe.matmul(ps, wqk[:, k, :], hT[:, :], start=True, stop=True))
                value, part = qk32[:, k, :], qk_parts[:, k, 0, :]
                wait(act, e, wqk_ok, last.get("qk32"), *last.get("parts_read", ()))
                bias, scale = ((bq_scaled[:, 0:1], D ** -0.5), (cols[:, 1:2], 1.0))[k]
                for dst in (value, part):
                    e = by_act(act.activation(dst, ps, ACT.Identity, bias=bias, scale=scale))
                bank_free[n] = (e,)
                wait(sub, e)
                rest_ok[k] = subtract(qk_rest[:, k, :], value, part)
                load_parts(k, 0, e)
                yield
            last["qk32"] = rest_ok[1]
            n, ps = bank()
            for i in range(NB):
                for m in range(2):
                    eV = by_pe(pe.matmul(ps[BLK * m:BLK * (m + 1), BLK * i:BLK * (i + 1)],
                                         hT[:, BLK * i:BLK * (i + 1)],
                                         w_in[:, 2, :].rearrange("c (p m d) -> c m p d", m=2, d=D)[:, m, :, :],
                                         start=True, stop=True))
            last["hT"] = eV
            for m, eng in ((0, act), (1, dve)):
                wait(eng, eV, vals_ok[b % KBUF], last.get(("vals", b % KBUF)))
                dst = vals[b % KBUF][BLK * m:BLK * (m + 1), :, :, 16 * m:16 * m + D]
                src = ps[BLK * m:BLK * (m + 1), :].rearrange("p (i h d) -> p i h d", i=NB, d=D)
                if m == 0:
                    v0 = by_act(act.copy(dst, src))
                else:
                    wait(dve, v0)
                    v1 = by_dve(dve.tensor_copy(dst, src))
            bank_free[n] = vals_in[b] = (v0, v1)
            yield
            for k in range(2):
                value, part = qk_rest[:, k, :], qk_parts[:, k, 1, :]
                wait(act, rest_ok[k])
                e = by_act(act.copy(part, value))
                load_parts(k, 1, e)
                wait(sub, e)
                e = subtract(qk_parts[:, k, 2, :], value, part)
                load_parts(k, 2, e)
                yield
            last["parts_read"] = ops_in[b, 0], ops_in[b, 1], ops_in.get((b, 2))

        vals_in, ops_in, maxima_in = {}, {}, {}

        def window(i):
            lo, hi = max(i - REACH, 0), min(i + REACH + 1, NB)
            return lo, hi, BLK * (lo - i + REACH), BLK * (hi - i + REACH)

        def max_scores(n, u):
            b, g = divmod(n, NG)
            pp, i2 = divmod(u, NB // 2)
            pair = GP * g + pp
            i = 2 * i2
            w0 = REACH - i - 1 if i < REACH else 0
            w1 = NB - i + REACH - 1 if i + 1 >= NB - REACH else WIN - 1
            b0 = 0 if i < REACH else 1
            b1 = 3 if i + 1 >= NB - REACH else 2
            k, ps = slot()
            wait(pe, ops_in[b, 0], ops_in[b, 1], ops_in.get((b, 2)), ones_in[b % KBUF], band_ok, identB_ok)
            for m in range(2):
                wide = ps[:, m, 0:WIN * BLK].rearrange("p (w s) -> p w s", w=WIN)
                by_pe(pe.matmul(wide[:, w0:w1 + 1:w1 - w0, :], identB[:, :], band[:, b0:b1 + 1:b1 - b0, :],
                                start=True, stop=False, skip_group_check=True))
            for m in range(2):
                for j in range(2):
                    lo, hi, c0, c1 = window(i + j)
                    e = by_pe(pe.matmul(ps[BLK * j:BLK * (j + 1), m, c0:c1], q_ops[b][:, pair, BLK * (i + j):BLK * (i + j + 1)],
                                        k_ops[b % KBUF][:, m, pair, BLK * lo:BLK * hi], start=False, stop=True,
                                        skip_group_check=True))
            wait(dve, e, last.get(("neg_max", n % 2)))
            e = by_dve(dve.tensor_reduce(neg_max[:, n % 2, :, pp, i2], ps[:, :, BLK * w0:BLK * (w1 + 1)], AX.X, ALU.max,
                                         negate=True))
            slot_free[k] = (e,)
            return e

        def place_maxima(n, e):
            b, g = divmod(n, NG)
            nm = neg_max[:, n % 2, :, :, :].rearrange("p m a i -> p m (a i)")
            wait(dve, e, last.get("max_parts"))
            e = by_dve(dve.tensor_copy(max_parts[:, :, 0, :], nm))
            wait(dve, e)
            e = by_dve(dve.tensor_tensor(max_rest[:, :, :], nm, max_parts[:, :, 0, :], ALU.subtract))
            last[("neg_max", n % 2)] = e
            wait(dve, e)
            e = by_dve(dve.tensor_copy(max_parts[:, :, 1, :], max_rest[:, :, :]))
            wait(dve, e)
            e = by_dve(dve.tensor_tensor(max_parts[:, :, 2, :], max_rest[:, :, :], max_parts[:, :, 1, :], ALU.subtract))
            yield
            k, ps = bank()
            wait(pe, e)
            psb = ps[0:PARTS * GP * NB, 0:P // 2].bitcast(BF16)
            e = by_pe(pe.transpose(psb, max_parts[:, :, :, :].rearrange("p m a i -> p (m a i)"), identB[:, :]))
            last["max_parts"] = e
            wait(act, e, maxima_in.get(n - 2))
            e = by_act(act.copy(max_rows[:, n % 2, :], psb))
            bank_free[k] = (e,)
            wait(act, e)
            maxima_in[n] = done(act.dma_start(q_ops[b][ROWS:ROWS + MAX_ROWS, GP * g:GP * (g + 1), :],
                                             max_rows[:, n % 2, :]), s_max[n], 16)
            yield

        probs_free = {}
        probs_in = {}

        def exp_scores(s, pp):
            n, i = divmod(s, NB)
            b, g = divmod(n, NG)
            pair = GP * g + pp
            lo, hi, c0, c1 = window(i)
            k, ps = bank()
            wait(pe, maxima_in[n])
            masked = pp >= POOL_PAIRS
            w0, w1 = (0 if i >= REACH else None), (WIN - 1 if i < NB - REACH else None)
            wide = ps[:, 0:WIN * BLK].rearrange("p (w s) -> p w s", w=WIN)
            if not masked:
                pass
            elif w0 is not None and w1 is not None:
                by_pe(pe.matmul(wide[:, w0:w1 + 1:w1 - w0, :], identB[:, :], band[:, 1:3, :],
                                start=True, stop=False, skip_group_check=True))
            else:
                w = w1 if w0 is None else w0
                by_pe(pe.matmul(wide[:, w, :], identB[:, :], band[:, 1 if w1 is None else 2, :],
                                start=True, stop=False, skip_group_check=True))
            for m in range(2):
                e = by_pe(pe.matmul(ps[BLK * m:BLK * (m + 1), c0:c1],
                                    k_ops[b % KBUF][:, m, pair, BLK * i:BLK * (i + 1)],
                                    q_ops[b][:, pair, BLK * lo:BLK * hi], start=not masked, stop=True,
                                    skip_group_check=True))
            last[("k_ops", b % KBUF)] = e
            wait(act, e, probs_free.get(s - RING))
            e = by_act(act.activation(probs[:, s % RING, pp, c0:c1], ps[:, c0:c1], ACT.Exp))
            bank_free[k] = (e,)
            return e

        def mask_probs(s, e):
            i = s % NB
            wait(pool, e)
            for m in (0, 1) if s % 2 else (1, 0):
                for w, sign in ((0, 1), (WIN - 1, -1)):
                    if not (i >= REACH if w == 0 else i < NB - REACH):
                        continue
                    t = probs[BLK * m:BLK * (m + 1), s % RING, 0:POOL_PAIRS, w * BLK:(w + 1) * BLK]
                    pool_from(BLK * m)
                    e = by_pool(pool.affine_select(out=t, in_=t, compare_op=ALU.is_ge, fill=0.0, base=0,
                                                   pattern=[[0, POOL_PAIRS], [sign, BLK]], channel_multiplier=-sign))
            return e

        def weighted_sums(s):
            n, i = divmod(s, NB)
            b, g = divmod(n, NG)
            lo, hi, c0, c1 = window(i)
            wait(pe, *probs_in[s], *vals_in[b])
            if i == 0:
                wait(pe, last.get("ps_sum"))
            for pp in range(GP):
                e = by_pe(pe.matmul(ps_sum[VW * pp:VW * (pp + 1), BLK * lo:BLK * hi], vals[b % KBUF][:, i, GP * g + pp, :],
                                    probs[:, s % RING, pp, c0:c1], start=(i == 0), stop=(i == NB - 1),
                                    skip_group_check=True))
            probs_free[s] = last[("vals", b % KBUF)] = e
            if i == NB - 1:
                wait(act, e, last.get(("sums_T", n % 2)))
                last["ps_sum"] = by_act(act.copy(sums_T[:, n % 2, :], ps_sum[:, :]))
                return last["ps_sum"]

        def normalise(n, e):
            b, g = divmod(n, NG)
            k, ps, e = transposed(e, lambda t: sums_T[:, n % 2, t * P:(t + 1) * P])
            last[("sums_T", n % 2)] = e
            sums = ps.rearrange("p (t h w) -> p t h w", t=NT, w=16)
            wait(dve, e, last.get("o_tok") if g == 0 else None)
            e = by_dve(dve.reciprocal(inv[:, n % 2, :, :], sums[:, :, :, D]))
            wait(dve, e)
            dst = o_tok[:, :, :].rearrange("p t (g h d) -> p t g h d", g=NG, d=D)[:, :, g, :, :]
            e = by_dve(dve.tensor_tensor(dst, sums[:, :, :, 0:D],
                                         inv[:, n % 2, :, :].unsqueeze(3).to_broadcast([P, NT, 2 * GP, D]), ALU.mult))
            bank_free[k] = (e,)
            normalised[n] = e
            yield

        normalised = {}

        def finish(b):
            xb = xt[:, NT * b:NT * (b + 1), :]
            hurried = b == B - 1
            n, ps, e = transposed(normalised[NG * b + NG - 1], lambda t: o_tok[:, t, :])
            last["o_tok"] = e
            wait(pool, xn_ok[b], gated["w"])
            pool_from(0)
            biased = by_pool(pool.tensor_tensor(xb, xb, bo_gated[:, b, :].unsqueeze(1).to_broadcast([P, NT, E]), ALU.add))
            wait(act, e, last.get("o_T"), small)
            e = by_act(act.activation(o_T[:, :], ps, ACT.Identity, bias=cols[:, 2:3]))
            bank_free[n] = (e,)
            yield
            n, ps = bank()
            wait(pe, e, gated["w"])
            for t in range(NT):
                e = by_pe(pe.matmul(ps[:, t * P:(t + 1) * P], o_T[:, t * P:(t + 1) * P], wo_gated[:, b, :],
                                    start=True, stop=True))
            last["o_T"] = e
            wait(dve, e, biased)
            e = by_dve(dve.tensor_tensor(xb, ps.rearrange("p (t e) -> p t e", t=NT), xb, ALU.add))
            bank_free[n] = (e,)
            yield
            wait(dve, e)
            x1_ok = e
            yield from layer_norm(b, hurried)
            n, ps, e = transposed(xn_ok[b], lambda t: xn[:, t, :])
            last["xn"] = e
            wait(act, e, h2_zero, last.get("h2"))
            h2_ok = by_act(act.activation(h2[:, 1:1 + S], ps, ACT.Identity, bias=modT[:, 2, b:b + 1],
                                          scale=modT[:, 3, b:b + 1]))
            bank_free[n] = (h2_ok,)
            engine, by = (dve, by_dve) if hurried else (pool, by_pool)
            wait(engine, h2_ok, last.get("h2_diff"))
            if not hurried:
                pool_from(0)
            e = by(engine.tensor_tensor(h2_diff[:, :], h2[:, 1:1 + S], h2[:, 0:S], ALU.subtract))
            yield
            yield
            wait(dve, e, small, last.get("mixed"))
            for k in range(2):
                mix_ok = by_dve(dve.scalar_tensor_tensor(mixed[:, k, :], h2_diff[:, :], cols[:, 3 + k:4 + k],
                                                         h2[:, 0:S], ALU.mult, ALU.add))
            last["h2"] = last["h2_diff"] = mix_ok
            yield
            n, ps = bank()
            wait(pe, mix_ok, gated["w"])
            for t in range(NT):
                e = by_pe(pe.matmul(ps[:, t * P:(t + 1) * P], mixed[:, 0, t * P:(t + 1) * P], wT[:, 0, :],
                                    start=True, stop=True))
            wait(act, e, last.get("gate_r"))
            e = by_act(act.activation(gate_r[:, :, :].rearrange("p t e -> p (t e)"), ps, ACT.Tanh, scale=0.5))
            bank_free[n] = (e,)
            yield
            n, ps = bank()
            e = by_pe(pe.matmul(ps, wT[:, 1, :], mixed[:, 1, :], start=True, stop=True))
            last["mixed"] = e
            wait(act, e, last.get("k_relu"))
            e = by_act(act.activation(k_relu[:, :], ps, ACT.Relu))
            bank_free[n] = (e,)
            yield
            wait(act, e, last.get("k_sq"))
            ksq_ok = by_act(act.square(k_sq[:, :], k_relu[:, :]))
            last["k_relu"] = ksq_ok
            yield
            n, ps = bank()
            wait(pe, ksq_ok)
            for t in range(NT):
                e = by_pe(pe.matmul(ps[:, t * P:(t + 1) * P], k_sq[:, t * P:(t + 1) * P], wv_gated[:, b, :],
                                    start=True, stop=True))
            last["k_sq"] = e
            wait(dve, e, last.get("y2"))
            e = by_dve(dve.scalar_tensor_tensor(y2[:, :, :].rearrange("p t e -> p (t e)"),
                                                gate_r[:, :, :].rearrange("p t e -> p (t e)"), 1.0, ps,
                                                ALU.add, ALU.mult))
            bank_free[n] = (e,)
            last["gate_r"] = e
            wait(engine, e, x1_ok)
            if not hurried:
                pool_from(0)
            e = by(engine.tensor_tensor(xb, xb, y2[:, :, :], ALU.add))
            last["y2"] = e
            wait(sp, e)
            stored[0] = done(sp.dma_start(out[b].rearrange("(t p) e -> p t e", p=P), xb), s_out, 16)
            yield

        stored = [None]

        def run(steps):
            for _ in steps:
                pass

        LAG = 2
        LEAD = 4
        UNITS = GP * NB // 2
        NGROUPS = B * NG
        PREPARE = NB
        run(prepare(0))
        max_done = {}

        def max_step(q):
            n, u = divmod(q, UNITS)
            if n >= NGROUPS:
                return
            e = max_scores(n, u)
            if u == UNITS - 1:
                placing.append(place_maxima(n, e))

        def clear(b):
            if b < KBUF:
                clear_vals(b)
                yield
                pool_from(0)
                clear_k(b)
                load_ones(b)
                yield
            pool_from(0)
            q_clear[b] = by_pool(pool.memset(words(q_ops[b][:, :, :]), 0.0))
            yield

        def step(queue):
            if queue and next(queue[0], "end") == "end":
                queue.pop(0)

        placing = []
        preparing, finishing = [prepare(1)], []
        step(preparing)
        run(clear(1))
        run(gates_and_gated_weights())
        for q in range(UNITS):
            max_step(q)
            if q % 2:
                step(preparing)
        while placing:
            step(placing)
        while preparing:
            step(preparing)
        for b in range(2, B):
            run(clear(b))
        for q in range(UNITS, UNITS + 2 * LEAD):
            max_step(q)
        finished = []
        for s in range(STEPS + LAG):
            n, i = divmod(s, NB)
            q = UNITS + 2 * (s + LEAD)
            e = None
            for pp in range(GP):
                if s < STEPS:
                    e = exp_scores(s, pp)
                    if pp == POOL_PAIRS - 1:
                        masked = mask_probs(s, e)
                if pp == 1:
                    max_step(q)
            if s < STEPS:
                probs_in[s] = e, masked
            step(placing)
            step(preparing)
            step(finishing)
            if finished and i == 3:
                m, e = finished.pop(0)
                run(normalise(m, e))
                if m % NG == NG - 1:
                    finishing.append(finish(m // NG))
            if s % (NG * NB) == PREPARE and s // (NG * NB) + 2 < B:
                preparing.append(prepare(s // (NG * NB) + 2))
            max_step(q + 1)
            if s >= LAG:
                e = weighted_sums(s - LAG)
                if e is not None:
                    m = (s - LAG) // NB
                    finished.append((m, e))
        for m, e in finished:
            run(normalise(m, e))
            if m % NG == NG - 1:
                finishing.append(finish(m // NG))
        for t in finishing:
            run(t)
        wait(sp, stored[0])


_INS = ['L0_attn_x', 'L0_attn_Wq', 'L0_attn_bq', 'L0_attn_Wk', 'L0_attn_bk', 'L0_attn_Wv', 'L0_attn_bv',
        'L0_attn_Wo', 'L0_attn_bo', 'L0_ffn_W_r', 'L0_ffn_W_k', 'L0_ffn_W_v', 'L0_ffn_mu_r', 'L0_ffn_mu_k',
        'L0_c', 'L0_wmod']


def kernel(**inputs):
    import numpy as _np
    import concourse.bacc as _bacc
    from concourse import mybir as _mybir
    from concourse.bass_utils import run_bass_kernel_spmd as _run

    nc = _bacc.Bacc("TRN2", target_bir_lowering=False, num_devices=1)
    arrays, args = {}, []
    for name in _INS:
        a = _np.ascontiguousarray(inputs[name])
        arrays[f"in_{name}_dram"] = a
        args.append(nc.dram_tensor(f"in_{name}_dram", a.shape, _mybir.dt.from_np(a.dtype), kind="ExternalInput").ap())
    shape = inputs['L0_attn_x'].shape
    args.append(nc.dram_tensor("out_0_dram", shape, _mybir.dt.float32, kind="ExternalOutput").ap())
    adaln_block(nc, *args)
    r = _run(nc, [arrays], core_ids=[0])
    return r.results[0]["out_0_dram"]
```

```python
from contextlib import ExitStack

import concourse.bass as bass
from concourse import mybir

F32 = mybir.dt.float32
BF16 = mybir.dt.bfloat16
ACT = mybir.ActivationFunctionType
ALU = mybir.AluOpType
AX = mybir.AxisListType

P = 128
EPS = 1e-5
GATE_FLOOR = 0.25
MASKED = -1e30


def adaln_block(nc, x, Wq, bq, Wk, bk, Wv, bv, Wo, bo, W_r, W_k, W_v, mu_r, mu_k, c, wmod, out):
    B, S, E = x.shape
    D = 8
    NT = S // P
    BLK = 64
    NB = S // BLK
    REACH = P // BLK
    WIN = 2 * REACH + 1
    PAIRS = E // D // 2
    GP = 4
    NG = PAIRS // GP
    NGROUPS = B * NG
    STEPS = NGROUPS * NB
    PARTS = 3
    PRODUCTS = [(0, 0), (0, 1), (1, 0), (1, 1), (0, 2), (2, 0)]
    ROWS = len(PRODUCTS) * 2 * D
    MAX_ROWS = 2 * PARTS
    POOL_PAIRS = 3
    KBUF = 3
    VW = 32
    assert E == P and S % P == 0 and NG * GP == PAIRS and GP * VW == P

    ctx = ExitStack()
    with ctx:
        def sb(name, shape, dt=F32):
            return ctx.enter_context(nc.sbuf_tensor(name, shape, dt))

        def sem(name):
            return ctx.enter_context(nc.semaphore(name))

        pe, dve, act, pool, sp = nc.tensor, nc.vector, nc.scalar, nc.gpsimd, nc.sync

        s_pe, s_dve, s_act, s_pool = sem("s_pe"), sem("s_dve"), sem("s_act"), sem("s_pool")
        count, seen = {}, {}

        def done(instruction, semaphore, by=1):
            instruction.then_inc(semaphore, by)
            count[id(semaphore)] = count.get(id(semaphore), 0) + by
            return semaphore, count[id(semaphore)]

        def wait(engine, *events):
            for event in events:
                if event is None:
                    continue
                semaphore, value = event
                key = (id(engine), id(semaphore))
                if seen.get(key, 0) < value:
                    engine.wait_ge(semaphore, value)
                    seen[key] = value

        def by_pe(i):
            return done(i, s_pe)

        def by_dve(i):
            return done(i, s_dve)

        def by_act(i):
            return done(i, s_act)

        def by_pool(i):
            return done(i, s_pool)

        pool_start = [0]

        def pool_from(partition):
            if pool_start[0] != partition:
                wait(pool, (s_pool, count[id(s_pool)]))
                pool_start[0] = partition

        xt = sb("xt", [P, B * NT, E])
        w_in = sb("w_in", [P, 7, E])
        wqk = sb("wqk", [P, 2, E])
        wT = sb("wT", [P, 3, E])
        wo_gated = sb("wo_gated", [P, B, E])
        wv_gated = sb("wv_gated", [P, B, E])
        wmod_sb = sb("wmod_sb", [P, 6 * E])
        cols = sb("cols", [P, 5])
        bq_scaled = sb("bq_scaled", [P, 1])
        bo_row = sb("bo_row", [1, E])
        ones_row = sb("ones_row", [1, P])
        c_sb = sb("c_sb", [B, E])
        c_tmp = sb("c_tmp", [B, 3, E])
        siluT = sb("siluT", [P, B])
        modT = sb("modT", [P, 4, B])
        gates = sb("gates", [P, B, 2, E])
        bo_gated = sb("bo_gated", [P, B, E])
        identF = sb("identF", [P, P])
        identB = sb("identB", [P, P], BF16)
        band = sb("band", [P, 4, BLK], BF16)
        minus_half = sb("minus_half", [P, NT])
        warm = sb("warm", [P, 1])
        zero = sb("zero", [P, 1])

        stats = sb("stats", [P, 2, NT, 6])
        mean_var = sb("mean_var", [P, 2, NT, 2])
        var_eps = sb("var_eps", [P, 2, NT])
        rstd = sb("rstd", [P, 2, NT])
        mean_rstd = sb("mean_rstd", [P, 2, NT])
        neg_mean_rstd = sb("neg_mean_rstd", [P, 2, NT])
        xn = sb("xn", [P, 2, NT, E])
        hT = sb("hT", [P, S])
        qk32 = sb("qk32", [P, 2, S])
        qk_rest = sb("qk_rest", [P, 2, S])
        qk_parts_of = [sb(f"qk_parts{b}", [P, 2, PARTS, S], BF16) for b in range(2)]
        q_ops = [sb(f"q_ops{b}", [P, PAIRS, S], BF16) for b in range(B)]
        k_ops = [sb(f"k_ops{b}", [P, 2, PAIRS, S], BF16) for b in range(KBUF)]
        vals = [sb(f"vals{b}", [P, NB, PAIRS, VW]) for b in range(KBUF)]
        neg_max = sb("neg_max", [P, 2, NB // 2, 2, GP])
        max_rest = sb("max_rest", [P, 2, NB // 4, 2, GP])
        max_parts = sb("max_parts", [P, 2, NB // 4, 2, PARTS, GP], BF16)
        max_ones = sb("max_ones", [MAX_ROWS, 2, S], BF16)
        max_rows = sb("max_rows", [PARTS * GP * NB // 2, 2, P], BF16)
        RING = 4
        probs = sb("probs", [P, RING, GP, WIN * BLK])
        sums_T = sb("sums_T", [P, 2, S])
        inv = sb("inv", [P, 2, NT, 2 * GP])
        o_tok = sb("o_tok", [P, NT, E])
        silu_wide = o_tok[:, 0:B, :]
        o_T = sb("o_T", [P, S])
        h2 = sb("h2", [P, 1 + S])
        h2_diff = sb("h2_diff", [P, S])
        mixed = sb("mixed", [P, 2, S])
        gate_r = sb("gate_r", [P, NT, E])
        k_relu = sb("k_relu", [P, S])
        k_sq = sb("k_sq", [P, S])
        y2 = k_relu[:, :].rearrange("p (t e) -> p t e", t=NT)

        ps_work = ctx.enter_context(nc.psum_tensor("ps_work", [P, 2, 2, 512], F32))
        ps_exp = ctx.enter_context(nc.psum_tensor("ps_exp", [P, 3, 512], F32))
        ps_sum = ctx.enter_context(nc.psum_tensor("ps_sum", [P, 512], F32))

        s_x = [sem(f"s_x{b}") for b in range(B)]
        s_c, s_wmod, s_qkv, s_mix, s_small, s_out = (sem(n) for n in
                                                       ("s_c", "s_wmod", "s_qkv", "s_mix", "s_small", "s_out"))
        s_q = [sem(f"s_q{b}") for b in range(B)]
        s_k = [sem(f"s_k{b}") for b in range(B)]
        s_k_second = sem("s_k_second")
        s_ones = [sem(f"s_ones{b}") for b in range(KBUF)]
        s_max = [[sem(f"s_max{n}_{h}") for h in range(2)] for n in range(NGROUPS)]

        def load_x(b):
            return done(sp.dma_start(xt[:, NT * b:NT * (b + 1), :], x[b].rearrange("(t p) e -> p t e", p=P)), s_x[b], 16)

        c_in = done(act.dma_start(c_sb[:, :], c), s_c, 16)
        x_in = {0: load_x(0)}
        wmod_in = done(sp.dma_start(wmod_sb[:, :], wmod), s_wmod, 16)
        for n, w in enumerate((Wq, Wk, Wv)):
            qkv_in = done(sp.dma_start(w_in[:, n, :], w), s_qkv, 16)
        x_in[1] = load_x(1)
        with nc.allow_non_contiguous_dma(reason="bias columns, 128 elements each"):
            for n, v in enumerate((bq, bk)):
                for m in range(2):
                    small = done(sp.dma_start(cols[BLK * m:BLK * (m + 1), n:n + 1],
                                               v.rearrange("(p m d) -> m d p", m=2, d=D)[m]), s_small, 16)
            for n, v in enumerate((bv, mu_r, mu_k)):
                small = done(sp.dma_start(cols[:, 2 + n:3 + n], v.rearrange("(p a) -> p a", a=1)), s_small, 16)
        small = done(sp.dma_start(bo_row[:, :], bo.rearrange("(a d) -> a d", a=1)), s_small, 16)
        for n, w in enumerate((Wo, W_r, W_k, W_v)):
            mix_in = done(sp.dma_start(w_in[:, 3 + n, :], w), s_mix, 16)
        for b in range(2, B):
            x_in[b] = load_x(b)

        q_clear, k_clear, vals_ok, ones_in = {}, {}, {}, {}

        def words(t):
            return t.rearrange("p a s -> p (a s)").bitcast(F32)

        def clear(words_of_buffer, by_scalar):
            if by_scalar:
                return by_act(act.copy(words_of_buffer, zero[:, :].to_broadcast([P, PAIRS * S // 2])))
            return by_pool(pool.memset(words_of_buffer, 0.0))

        def clear_q(b, by_scalar=False):
            q_clear[b] = clear(words(q_ops[b][:, :, :]), by_scalar)

        def clear_k(b, by_scalar=False):
            for m in range(2):
                k_clear[b] = clear(words(k_ops[b][:, m, :, :]), by_scalar)

        def load_ones(b):
            wait(sp, k_clear[b], max_ones_ok)
            for m in range(2):
                ones_in[b] = done(sp.dma_start(k_ops[b][ROWS:ROWS + MAX_ROWS, m, :, :],
                                               max_ones[:, m, :].unsqueeze(1).to_broadcast([MAX_ROWS, PAIRS, S])),
                                  s_ones[b], 16)

        def clear_vals(b):
            pool_from(0)
            e = by_pool(pool.memset(vals[b][:, :, :, :], 0.0))
            wait(pool, e)
            for m in range(2):
                pool_from(BLK * m)
                vals_ok[b] = by_pool(pool.memset(vals[b][BLK * m:BLK * (m + 1), :, :, 16 * m + D:16 * m + D + 1], 1.0))

        by_pool(pool.memset(zero[:, :], 0.0))
        half_ok = by_pool(pool.memset(minus_half[:, :], -0.5))
        by_pool(pool.memset(identF[:, :], 0.0))
        zeroed = by_pool(pool.memset(band[:, :, :], 0.0))
        wait(pool, zeroed)
        identF_ok = by_pool(pool.affine_select(out=identF[:, :], in_=identF[:, :], compare_op=ALU.not_equal, fill=1.0,
                                               base=0, pattern=[[-1, P]], channel_multiplier=1))
        wait(act, half_ok)
        by_act(act.activation(warm[:, :], minus_half[:, 0:1], ACT.Exp))

        wait(act, c_in)
        exp_c = by_act(act.activation(c_tmp[:, 0, :], c_sb[:, :], ACT.Exp, scale=-1.0))
        clear_q(1, by_scalar=True)
        clear_k(1, by_scalar=True)

        ones_set = by_dve(dve.memset(ones_row[:, :], 1.0))
        h2_zero = by_dve(dve.memset(h2[:, 0:1], 0.0))
        wait(dve, identF_ok)
        identB_ok = by_dve(dve.tensor_copy(identB[:, :], identF[:, :]))

        gated, biased, normalised, xn_ok = {}, {}, {}, {}
        vals_in, ops_in, maxima_in, probs_in = {}, {}, {}, {}
        probs_free = {}
        last = {}
        stored = [None]
        ALL = range(NT)

        bank_free = [()] * 3
        bank_turn = [0]

        def bank():
            n = bank_turn[0] % 3
            bank_turn[0] += 1
            wait(pe, *bank_free[n])
            return n, ps_exp[:, n, :]

        slot_free = [(), ()]
        turn = [0]

        def slot():
            n = turn[0] % 2
            turn[0] += 1
            wait(pe, *slot_free[n])
            return n, ps_work[:, n, :, :]

        def gates_and_gated_weights():
            n, ps = slot()
            wait(pe, wide_ok)
            for b in range(B):
                e = by_pe(pe.matmul(ps[:, b // 2, (b % 2) * 2 * E:(b % 2 + 1) * 2 * E],
                                    silu_wide[:, b, :],
                                    wmod_sb[:, :].rearrange("p (k e) -> p k e", k=6)[:, 2::3, :], start=True, stop=True))
            last["o_tok"] = e
            gates_flat = gates[:, :, :, :].rearrange("p b k e -> p (b k e)")
            wait(act, e)
            raw_ok = by_act(act.copy(gates_flat, ps[:, :, :].rearrange("p a f -> p (a f)")))
            slot_free[n] = (raw_ok,)
            yield
            gate_sign, gate_size = (t[:, :, :].rearrange("p k s -> p (k s)") for t in (mixed, sums_T))
            wait(dve, raw_ok)
            e = by_dve(dve.tensor_scalar(gate_sign, gates_flat, 0.0, 0.5, ALU.is_ge, ALU.subtract))
            yield
            wait(dve, e)
            e = by_dve(dve.scalar_tensor_tensor(gate_size, gate_sign, 2.0, gates_flat, ALU.mult, ALU.mult))
            yield
            wait(dve, e)
            gates_ok = by_dve(dve.scalar_tensor_tensor(gates_flat, gate_size, GATE_FLOOR, gate_sign,
                                                       ALU.max, ALU.mult))
            last["mixed"] = last["sums_T", 0] = last["sums_T", 1] = gates_ok
            yield
            n, ps = slot()
            wait(pe, ones_set, small, mix_in)
            e = by_pe(pe.matmul(ps[:, 0, 0:E], ones_row[:, :], bo_row[:, :], start=True, stop=True))
            for k in range(3):
                eT = by_pe(pe.transpose(ps[:, 1, k * E:(k + 1) * E], w_in[:, 4 + k, :], identF[:, :]))
            wait(dve, e, eT, gates_ok, mix_in)
            by_dve(dve.scalar_tensor_tensor(bo_gated[:, :, :], gates[:, :, 0, :], 2.0,
                                            ps[:, 0, 0:E].unsqueeze(1).to_broadcast([P, B, E]), ALU.mult, ALU.mult))
            wait(act, eT)
            e = by_act(act.copy(wT[:, :, :], ps[:, 1, 0:3 * E].rearrange("p (k e) -> p k e", k=3)))
            wait(dve, e)
            slot_free[n] = (e, (s_dve, count[id(s_dve)]))
            yield
            by_dve(dve.scalar_tensor_tensor(wo_gated[:, :, :], gates[:, :, 0, :], 2.0,
                                            w_in[:, 3, :].unsqueeze(1).to_broadcast([P, B, E]), ALU.mult, ALU.mult))
            gated["w"] = by_dve(dve.tensor_tensor(wv_gated[:, :, :], gates[:, :, 1, :],
                                                  wT[:, 2, :].unsqueeze(1).to_broadcast([P, B, E]), ALU.mult))
            yield

        def layer_norm(b, half_of_block, hurried=False, tiles=ALL):
            u, ts = half_of_block, slice(tiles.start, tiles.stop)
            wait(dve, last.get(("rstd", u)), last.get(("xn_made", u)))
            for t in tiles:
                e = by_dve(dve.bn_stats(stats[:, u, t, :], xt[:, NT * b + t, :]))
                if t == NT // 2 - 1 and not hurried:
                    yield
            wait(dve, e)
            for t in tiles:
                e = by_dve(dve.bn_aggr(mean_var[:, u, t, :], stats[:, u, t, :]))
            wait(dve, e)
            e = by_dve(dve.tensor_scalar(var_eps[:, u, ts], mean_var[:, u, ts, 1], EPS, None, ALU.add))
            wait(pool, e, last.get(("xn_made", u)))
            pool_from(0)
            e = by_pool(pool.tensor_tensor(rstd[:, u, ts], var_eps[:, u, ts], minus_half[:, ts], ALU.pow))
            last["rstd", u] = e
            if hurried:
                yield
                wait(dve, e, last.get(("xn", u)))
                for t in tiles:
                    e = by_dve(dve.tensor_scalar(xn[:, u, t, :], xt[:, NT * b + t, :], mean_var[:, u, t, 0:1],
                                                 rstd[:, u, t:t + 1], ALU.subtract, ALU.mult))
            else:
                wait(pool, e)
                e = by_pool(pool.tensor_tensor(mean_rstd[:, u, :], mean_var[:, u, :, 0], rstd[:, u, :], ALU.mult))
                wait(pool, e)
                e = by_pool(pool.tensor_scalar(neg_mean_rstd[:, u, :], mean_rstd[:, u, :], -1.0, None, ALU.mult))
                yield
                yield
                wait(act, e, last.get(("xn", u)))
                for t in tiles:
                    e = by_act(act.activation(xn[:, u, t, :], xt[:, NT * b + t, :], ACT.Identity, scale=rstd[:, u, t:t + 1],
                                              bias=neg_mean_rstd[:, u, t:t + 1]))
                    if t == NT // 2 - 1:
                        yield
            last["xn_made", u] = xn_ok[b, u, tiles.start] = e
            yield

        def transposed(ready, source, tiles=ALL):
            n, ps = bank()
            wait(pe, ready)
            for t in tiles:
                e = by_pe(pe.transpose(ps[:, t * P:(t + 1) * P], source(t), identF[:, :]))
            return n, ps, e

        first_norm = layer_norm(0, 0, hurried=True)
        wait(dve, x_in[0])
        next(first_norm)
        pool_from(0)
        clear_q(0)
        clear_k(0)
        wait(dve, exp_c)
        e = by_dve(dve.tensor_scalar(c_tmp[:, 1, :], c_tmp[:, 0, :], 1.0, None, ALU.add))
        wait(dve, e)
        e = by_dve(dve.reciprocal(c_tmp[:, 2, :], c_tmp[:, 1, :]))
        wait(dve, e, c_in)
        silu_ok = by_dve(dve.tensor_tensor(c_tmp[:, 0, :], c_tmp[:, 2, :], c_sb[:, :], ALU.mult))
        n, ps = slot()
        wait(pe, silu_ok, identF_ok)
        e = by_pe(pe.transpose(ps[:, 0, 0:B], c_tmp[:, 0, :], identF[0:B, 0:B]))
        wait(dve, e)
        siluT_ok = by_dve(dve.tensor_copy(siluT[:, :], ps[:, 0, 0:B]))
        slot_free[n] = (siluT_ok,)
        wait(dve, siluT_ok)
        next(first_norm)
        n, ps = slot()
        wait(pe, siluT_ok, wmod_in)
        for k, j in enumerate((0, 1, 3, 4)):
            e = by_pe(pe.matmul(ps[:, 0, k * B:(k + 1) * B], wmod_sb[:, j * E:(j + 1) * E], siluT[:, :],
                                start=True, stop=True))
        mod_ps = ps[:, 0, 0:4 * B].rearrange("p (k b) -> p k b", k=4)
        wait(dve, e)
        by_dve(dve.tensor_copy(modT[:, 0::2, :], mod_ps[:, 0::2, :]))
        modT_ok = by_dve(dve.tensor_scalar(modT[:, 1::2, :], mod_ps[:, 1::2, :], 1.0, None, ALU.add))
        slot_free[n] = (modT_ok,)
        wait(dve, qkv_in)
        for k in range(2):
            for m in range(2):
                wqk_ok = by_dve(dve.tensor_copy(
                    wqk[:, k, BLK * m:BLK * (m + 1)].rearrange("c (d p) -> c d p", d=D),
                    w_in[:, k, :].rearrange("c (p m d) -> c m d p", m=2, d=D)[:, m, :, :]))
        wait(dve, small)
        wqk_ok = by_dve(dve.tensor_scalar(bq_scaled[:, :], cols[:, 0:1], D ** -0.5, None, ALU.mult))
        wide_ok = by_dve(dve.tensor_copy(silu_wide[:, :, :], siluT[:, :].unsqueeze(2).to_broadcast([P, B, P])))

        def prepare(b):
            qk_parts = qk_parts_of[b % 2]
            if b:
                wait(dve, x_in[b])
                yield from layer_norm(b, 0, hurried=b == 1)
            n, ps, e = transposed(xn_ok[b, 0, 0], lambda t: xn[:, 0, t, :])
            last["xn", 0] = e
            wait(act, e, modT_ok, last.get("hT"))
            hT_ok = by_act(act.activation(hT[:, :], ps, ACT.Identity, bias=modT[:, 0, b:b + 1],
                                          scale=modT[:, 1, b:b + 1]))
            bank_free[n] = (hT_ok,)
            yield
            sub, by_sub = (dve, by_dve) if b == 0 else (pool, by_pool)

            def subtract(rest, value, part):
                if b:
                    pool_from(0)
                return by_sub(sub.tensor_tensor(rest, value, part, ALU.subtract))

            def load_parts(k, part, ready):
                rows = [2 * D * r for r, product in enumerate(PRODUCTS) if product[k] == part]
                if k == 0:
                    wait(sp, ready, q_clear[b])
                    for r in rows:
                        ops_in[b, 0] = done(sp.dma_start(q_ops[b][r:r + 2 * D, :, :], qk_parts[:, 0, part, :]), s_q[b], 16)
                    return
                for m in range(2):
                    second = b == 0 and m == 1
                    engine = pool if second else sp
                    wait(engine, ready, k_clear[b % KBUF], last.get(("k_ops", b % KBUF)))
                    for r in rows:
                        ops_in[b, 2 if second else 1] = done(
                            engine.dma_start(k_ops[b % KBUF][r + D * m:r + D * (m + 1), m, :, :],
                                             qk_parts[BLK * m:BLK * (m + 1), 1, part, :]),
                            s_k_second if second else s_k[b], 16)

            rest_ok = [None, None]
            for k in range(2):
                n, ps = bank()
                wait(pe, hT_ok, wqk_ok, qkv_in)
                e = by_pe(pe.matmul(ps, wqk[:, k, :], hT[:, :], start=True, stop=True))
                value, part = qk32[:, k, :], qk_parts[:, k, 0, :]
                wait(act, e, wqk_ok, last.get("qk32"), *last.get(("parts_read", b % 2), ()))
                bias, scale = ((bq_scaled[:, 0:1], D ** -0.5), (cols[:, 1:2], 1.0))[k]
                for dst in (value, part):
                    e = by_act(act.activation(dst, ps, ACT.Identity, bias=bias, scale=scale))
                bank_free[n] = (e,)
                wait(sub, e, last.get("qk_rest"))
                rest_ok[k] = subtract(qk_rest[:, k, :], value, part)
                load_parts(k, 0, e)
                yield
            last["qk32"] = rest_ok[1]
            n, ps = bank()
            for i in range(NB):
                for m in range(2):
                    eV = by_pe(pe.matmul(ps[BLK * m:BLK * (m + 1), BLK * i:BLK * (i + 1)],
                                         hT[:, BLK * i:BLK * (i + 1)],
                                         w_in[:, 2, :].rearrange("c (p m d) -> c m p d", m=2, d=D)[:, m, :, :],
                                         start=True, stop=True))
            last["hT"] = eV
            for m, eng in ((0, act), (1, dve)):
                wait(eng, eV, vals_ok[b % KBUF], last.get(("vals", b % KBUF)))
                dst = vals[b % KBUF][BLK * m:BLK * (m + 1), :, :, 16 * m:16 * m + D]
                src = ps[BLK * m:BLK * (m + 1), :].rearrange("p (i h d) -> p i h d", i=NB, d=D)
                if m == 0:
                    v0 = by_act(act.copy(dst, src))
                else:
                    wait(dve, v0)
                    v1 = by_dve(dve.tensor_copy(dst, src))
            bank_free[n] = vals_in[b] = (v0, v1)
            yield
            for k in range(2):
                value, part = qk_rest[:, k, :], qk_parts[:, k, 1, :]
                wait(act, rest_ok[k])
                e = by_act(act.copy(part, value))
                load_parts(k, 1, e)
                wait(sub, e)
                e = subtract(qk_parts[:, k, 2, :], value, part)
                load_parts(k, 2, e)
                last["qk_rest"] = e
                last["parts_read", b % 2] = ops_in[b, 0], ops_in[b, 1], ops_in.get((b, 2))
                yield

        def window(i):
            lo, hi = max(i - REACH, 0), min(i + REACH + 1, NB)
            return lo, hi, BLK * (lo - i + REACH), BLK * (hi - i + REACH)

        def max_scores(n, u):
            b, g = divmod(n, NG)
            i2, pp = divmod(u, GP)
            pair = GP * g + pp
            i = 2 * i2
            w0 = REACH - i - 1 if i < REACH else 0
            w1 = NB - i + REACH - 1 if i + 1 >= NB - REACH else WIN - 1
            b0 = 0 if i < REACH else 1
            b1 = 3 if i + 1 >= NB - REACH else 2
            k, ps = slot()
            wait(pe, ops_in[b, 0], ops_in[b, 1], ops_in.get((b, 2)), ones_in[b % KBUF], band_ok, identB_ok)
            for m in range(2):
                wide = ps[:, m, 0:WIN * BLK].rearrange("p (w s) -> p w s", w=WIN)
                by_pe(pe.matmul(wide[:, w0:w1 + 1:w1 - w0, :], identB[:, :], band[:, b0:b1 + 1:b1 - b0, :],
                                start=True, stop=False, skip_group_check=True))
            for m in range(2):
                for j in range(2):
                    lo, hi, c0, c1 = window(i + j)
                    e = by_pe(pe.matmul(ps[BLK * j:BLK * (j + 1), m, c0:c1], q_ops[b][:, pair, BLK * (i + j):BLK * (i + j + 1)],
                                        k_ops[b % KBUF][:, m, pair, BLK * lo:BLK * hi], start=False, stop=True,
                                        skip_group_check=True))
            wait(dve, e, last.get(("neg_max", n % 2)))
            e = by_dve(dve.tensor_reduce(neg_max[:, n % 2, i2, :, pp], ps[:, :, BLK * w0:BLK * (w1 + 1)], AX.X, ALU.max,
                                         negate=True))
            slot_free[k] = (e,)
            return e

        def place_maxima(n, h, e):
            b, g = divmod(n, NG)
            two_blocks = NB // 4
            nm = neg_max[:, n % 2, two_blocks * h:two_blocks * (h + 1), :, :]
            rest = max_rest[:, h, :, :, :]
            parts = [max_parts[:, h, :, :, part, :] for part in range(PARTS)]
            wait(dve, e, last.get(("max_parts", h)))
            e = by_dve(dve.tensor_copy(parts[0], nm))
            wait(dve, e)
            e = by_dve(dve.tensor_tensor(rest, nm, parts[0], ALU.subtract))
            last[("neg_max", n % 2)] = e
            wait(dve, e)
            e = by_dve(dve.tensor_copy(parts[1], rest))
            wait(dve, e)
            e = by_dve(dve.tensor_tensor(parts[2], rest, parts[1], ALU.subtract))
            yield
            k, ps = bank()
            wait(pe, e)
            psb = ps[0:two_blocks * MAX_ROWS * GP, 0:P // 2].bitcast(BF16)
            e = by_pe(pe.transpose(psb, max_parts[:, h, :, :, :, :].rearrange("p i m c a -> p (i m c a)"), identB[:, :]))
            last["max_parts", h] = e
            wait(act, e, maxima_in.get((n - 1, h)))
            e = by_act(act.copy(max_rows[:, h, :], psb))
            bank_free[k] = (e,)
            queue = act if n == 0 else sp
            wait(queue, e)
            rows = MAX_ROWS * GP
            for i in range(two_blocks):
                first = P * (two_blocks * h + i)
                maxima_in[n, h] = done(queue.dma_start(
                    q_ops[b][ROWS:ROWS + MAX_ROWS, GP * g:GP * (g + 1), first:first + P],
                    max_rows[rows * i:rows * (i + 1), h, :]), s_max[n][h], 16)
            yield

        def exp_scores(s, pp):
            n, i = divmod(s, NB)
            b, g = divmod(n, NG)
            pair = GP * g + pp
            lo, hi, c0, c1 = window(i)
            k, ps = bank()
            wait(pe, maxima_in[n, 0], maxima_in[n, 1] if hi > NB // 2 else None)
            masked = pp >= POOL_PAIRS
            w0, w1 = (0 if i >= REACH else None), (WIN - 1 if i < NB - REACH else None)
            wide = ps[:, 0:WIN * BLK].rearrange("p (w s) -> p w s", w=WIN)
            if not masked:
                pass
            elif w0 is not None and w1 is not None:
                by_pe(pe.matmul(wide[:, w0:w1 + 1:w1 - w0, :], identB[:, :], band[:, 1:3, :],
                                start=True, stop=False, skip_group_check=True))
            else:
                w = w1 if w0 is None else w0
                by_pe(pe.matmul(wide[:, w, :], identB[:, :], band[:, 1 if w1 is None else 2, :],
                                start=True, stop=False, skip_group_check=True))
            for m in range(2):
                e = by_pe(pe.matmul(ps[BLK * m:BLK * (m + 1), c0:c1],
                                    k_ops[b % KBUF][:, m, pair, BLK * i:BLK * (i + 1)],
                                    q_ops[b][:, pair, BLK * lo:BLK * hi], start=not masked, stop=True,
                                    skip_group_check=True))
            last[("k_ops", b % KBUF)] = e
            wait(act, e, probs_free.get(s - RING))
            e = by_act(act.activation(probs[:, s % RING, pp, c0:c1], ps[:, c0:c1], ACT.Exp))
            bank_free[k] = (e,)
            return e

        def mask_probs(s, e):
            i = s % NB
            wait(pool, e)
            for m in (0, 1) if s % 2 else (1, 0):
                for w, sign in ((0, 1), (WIN - 1, -1)):
                    if not (i >= REACH if w == 0 else i < NB - REACH):
                        continue
                    t = probs[BLK * m:BLK * (m + 1), s % RING, 0:POOL_PAIRS, w * BLK:(w + 1) * BLK]
                    pool_from(BLK * m)
                    e = by_pool(pool.affine_select(out=t, in_=t, compare_op=ALU.is_ge, fill=0.0, base=0,
                                                   pattern=[[0, POOL_PAIRS], [sign, BLK]], channel_multiplier=-sign))
            return e

        def weighted_sums(s):
            n, i = divmod(s, NB)
            b, g = divmod(n, NG)
            lo, hi, c0, c1 = window(i)
            wait(pe, *probs_in[s], *vals_in[b])
            if i == 0:
                wait(pe, last.get("ps_sum"))
            for pp in range(GP):
                e = by_pe(pe.matmul(ps_sum[VW * pp:VW * (pp + 1), BLK * lo:BLK * hi], vals[b % KBUF][:, i, GP * g + pp, :],
                                    probs[:, s % RING, pp, c0:c1], start=(i == 0), stop=(i == NB - 1),
                                    skip_group_check=True))
            probs_free[s] = last[("vals", b % KBUF)] = e
            half_done = n == NGROUPS - 1 and i == NB // 2 - 1 + REACH
            if half_done or i == NB - 1:
                tiles = range(NT // 2) if half_done else range(NT // 2, NT) if n == NGROUPS - 1 else ALL
                columns = slice(P * tiles.start, P * tiles.stop)
                wait(act, e, last.get(("sums_T", n % 2)))
                e = by_act(act.copy(sums_T[:, n % 2, columns], ps_sum[:, columns]))
                last["ps_sum"] = e
                if half_done:
                    wait(pe, e)
                return n, tiles, e

        def normalise(n, tiles, e):
            b, g = divmod(n, NG)
            ts, columns = slice(tiles.start, tiles.stop), slice(P * tiles.start, P * tiles.stop)
            k, ps, e = transposed(e, lambda t: sums_T[:, n % 2, t * P:(t + 1) * P], tiles)
            last[("sums_T", n % 2)] = e
            sums = ps[:, columns].rearrange("p (t h w) -> p t h w", t=len(tiles), w=16)
            wait(dve, e, last.get("o_tok") if g == 0 else None)
            e = by_dve(dve.reciprocal(inv[:, n % 2, ts, :], sums[:, :, :, D]))
            wait(dve, e)
            dst = o_tok[:, ts, :].rearrange("p t (g h d) -> p t g h d", g=NG, d=D)[:, :, g, :, :]
            e = by_dve(dve.tensor_tensor(dst, sums[:, :, :, 0:D],
                                         inv[:, n % 2, ts, :].unsqueeze(3).to_broadcast([P, len(tiles), 2 * GP, D]),
                                         ALU.mult))
            bank_free[k] = (e,)
            normalised[n, tiles.start] = e

        def add_bias(b):
            xb = xt[:, NT * b:NT * (b + 1), :]
            wait(pool, xn_ok[b, 0, 0], gated["w"])
            pool_from(0)
            biased[b] = by_pool(pool.tensor_tensor(xb, xb, bo_gated[:, b, :].unsqueeze(1).to_broadcast([P, NT, E]),
                                                   ALU.add))

        def finish(b, tiles=ALL):
            t0, t1 = tiles.start, tiles.stop
            ts, columns = slice(t0, t1), slice(P * t0, P * t1)
            xb = xt[:, NT * b + t0:NT * b + t1, :]
            hurried = b == B - 1
            n, ps, e = transposed(normalised[NG * b + NG - 1, t0], lambda t: o_tok[:, t, :], tiles)
            last["o_tok"] = e
            if b not in biased:
                add_bias(b)
            wait(act, e, last.get("o_T"), small)
            e = by_act(act.activation(o_T[:, columns], ps[:, columns], ACT.Identity, bias=cols[:, 2:3]))
            bank_free[n] = (e,)
            yield
            n, ps = bank()
            wait(pe, e, gated["w"])
            for t in tiles:
                e = by_pe(pe.matmul(ps[:, t * P:(t + 1) * P], o_T[:, t * P:(t + 1) * P], wo_gated[:, b, :],
                                    start=True, stop=True))
            last["o_T"] = e
            wait(dve, e, biased[b])
            e = by_dve(dve.tensor_tensor(xb, ps[:, columns].rearrange("p (t e) -> p t e", e=E), xb, ALU.add))
            bank_free[n] = (e,)
            yield
            wait(dve, e)
            x1_ok = e
            yield from layer_norm(b, 1, hurried, tiles)
            n, ps, e = transposed(xn_ok[b, 1, t0], lambda t: xn[:, 1, t, :], tiles)
            last["xn", 1] = e
            wait(act, e, h2_zero, last.get("h2"))
            h2_ok = by_act(act.activation(h2[:, 1 + P * t0:1 + P * t1], ps[:, columns], ACT.Identity, bias=modT[:, 2, b:b + 1],
                                          scale=modT[:, 3, b:b + 1]))
            bank_free[n] = (h2_ok,)
            engine, by = (dve, by_dve) if hurried else (pool, by_pool)
            wait(engine, h2_ok, last.get("h2_diff"))
            if not hurried:
                pool_from(0)
            e = by(engine.tensor_tensor(h2_diff[:, columns], h2[:, 1 + P * t0:1 + P * t1], h2[:, columns], ALU.subtract))
            yield
            yield
            wait(dve, e, small, last.get("mixed"))
            for k in range(2):
                mix_ok = by_dve(dve.scalar_tensor_tensor(mixed[:, k, columns], h2_diff[:, columns], cols[:, 3 + k:4 + k],
                                                         h2[:, columns], ALU.mult, ALU.add))
                if k == 0:
                    yield
            last["h2"] = last["h2_diff"] = mix_ok
            yield
            n, ps = bank()
            wait(pe, mix_ok, gated["w"])
            for t in tiles:
                e = by_pe(pe.matmul(ps[:, t * P:(t + 1) * P], mixed[:, 0, t * P:(t + 1) * P], wT[:, 0, :],
                                    start=True, stop=True))
            wait(act, e, last.get("gate_r"))
            e = by_act(act.activation(gate_r[:, ts, :].rearrange("p t e -> p (t e)"), ps[:, columns], ACT.Tanh, scale=0.5))
            bank_free[n] = (e,)
            yield
            n, ps = bank()
            e = by_pe(pe.matmul(ps[:, columns], wT[:, 1, :], mixed[:, 1, columns], start=True, stop=True))
            last["mixed"] = e
            wait(act, e, last.get("k_relu"), last.get("y2"))
            e = by_act(act.activation(k_relu[:, columns], ps[:, columns], ACT.Relu))
            bank_free[n] = (e,)
            yield
            wait(act, e, last.get("k_sq"))
            ksq_ok = by_act(act.square(k_sq[:, columns], k_relu[:, columns]))
            last["k_relu"] = ksq_ok
            yield
            n, ps = bank()
            wait(pe, ksq_ok)
            for t in tiles:
                e = by_pe(pe.matmul(ps[:, t * P:(t + 1) * P], k_sq[:, t * P:(t + 1) * P], wv_gated[:, b, :],
                                    start=True, stop=True))
            last["k_sq"] = e
            wait(dve, e, last.get("y2"))
            e = by_dve(dve.scalar_tensor_tensor(y2[:, ts, :].rearrange("p t e -> p (t e)"),
                                                gate_r[:, ts, :].rearrange("p t e -> p (t e)"), 1.0,
                                                ps[:, columns],
                                                ALU.add, ALU.mult))
            bank_free[n] = (e,)
            last["gate_r"] = e
            wait(engine, e, x1_ok)
            if not hurried:
                pool_from(0)
            e = by(engine.tensor_tensor(xb, xb, y2[:, ts, :], ALU.add))
            last["y2"] = e
            wait(sp, e)
            stored[0] = done(sp.dma_start(out[b].rearrange("(t p) e -> p t e", p=P)[:, ts, :], xb), s_out, 16)
            yield

        LAG = 2
        AHEAD = 7
        UNITS = GP * NB // 2
        PREPARE = NB

        def max_step(q):
            n, u = divmod(q, UNITS)
            if n >= NGROUPS:
                return
            e = max_scores(n, u)
            if u % (UNITS // 2) == UNITS // 2 - 1:
                placing.append(place_maxima(n, u // (UNITS // 2), e))

        def step(queue):
            if queue and next(queue[0], "end") == "end":
                queue.pop(0)

        first, second, gating = prepare(0), prepare(1), gates_and_gated_weights()
        placing, preparing, finishing = [], [], [gating]
        next(first)
        next(second)
        max_ones_set = by_pool(pool.memset(max_ones[:, :, :], 1.0))
        for m in range(2):
            rows = slice(BLK * m, BLK * (m + 1))
            pool_from(BLK * m)
            by_pool(pool.affine_select(out=band[rows, 1, :], in_=band[rows, 1, :], compare_op=ALU.is_ge, fill=MASKED,
                                       base=0, pattern=[[1, BLK]], channel_multiplier=-1))
            by_pool(pool.affine_select(out=band[rows, 2, :], in_=band[rows, 2, :], compare_op=ALU.is_ge,
                                       fill=MASKED, base=0, pattern=[[-1, BLK]], channel_multiplier=1))
            band_ok = by_pool(pool.memset(band[rows, 3 * m, :], MASKED))
        pool_from(0)
        wait(pool, max_ones_set)
        for m in range(2):
            sign = 1 if m else -1
            max_ones_ok = by_pool(pool.affine_select(
                out=max_ones[:, m, :], in_=max_ones[:, m, :], compare_op=ALU.is_ge, fill=0.0,
                base=-PARTS if m else PARTS - 1, pattern=[[0, S]], channel_multiplier=sign))
        load_ones(0)
        clear_vals(0)
        for generator in (first, second, first, first, first, first):
            next(generator, None)
        clear_vals(1)
        load_ones(1)
        for generator in (second, gating, second, second, gating, gating, second, second, second):
            next(generator, None)
        for b in range(2, B):
            if b < KBUF:
                clear_vals(b)
            pool_from(0)
            if b < KBUF:
                clear_k(b)
                load_ones(b)
            clear_q(b)
        for q in range(UNITS // 2):
            max_step(q)
        while placing:
            step(placing)
        for q in range(UNITS // 2, UNITS // 2 + AHEAD):
            max_step(q)
        q = UNITS // 2 + AHEAD
        finished = []
        for s in range(STEPS + LAG):
            n, i = divmod(s, NB)
            per_stage = 4 if s < 2 else 2
            e = None
            for pp in range(GP):
                if s < STEPS:
                    e = exp_scores(s, pp)
                    if pp == POOL_PAIRS - 1:
                        masked = mask_probs(s, e)
                if pp == 1:
                    for _ in range(per_stage // 2):
                        max_step(q)
                        q += 1
                    if s < 2:
                        step(placing)
            if s < STEPS:
                probs_in[s] = e, masked
            step(placing)
            step(preparing)
            step(finishing)
            if s == STEPS - NB:
                add_bias(B - 1)
            if finished and (i == 3 or s >= STEPS):
                m, tiles, e = finished.pop(0)
                normalise(m, tiles, e)
                if m % NG == NG - 1:
                    finishing.append(finish(m // NG, tiles))
            if s % (NG * NB) == PREPARE and s // (NG * NB) + 2 < B:
                preparing.append(prepare(s // (NG * NB) + 2))
            for _ in range(per_stage // 2):
                max_step(q)
                q += 1
            if s >= LAG:
                e = weighted_sums(s - LAG)
                if e is not None:
                    finished.append(e)
        for m, tiles, e in finished:
            normalise(m, tiles, e)
            finishing.append(finish(m // NG, tiles))
        while finishing:
            for steps in list(finishing):
                if next(steps, "end") == "end":
                    finishing.remove(steps)
        wait(sp, stored[0])


_INS = ['L0_attn_x', 'L0_attn_Wq', 'L0_attn_bq', 'L0_attn_Wk', 'L0_attn_bk', 'L0_attn_Wv', 'L0_attn_bv',
        'L0_attn_Wo', 'L0_attn_bo', 'L0_ffn_W_r', 'L0_ffn_W_k', 'L0_ffn_W_v', 'L0_ffn_mu_r', 'L0_ffn_mu_k',
        'L0_c', 'L0_wmod']


def kernel(**inputs):
    import numpy as _np
    import concourse.bacc as _bacc
    from concourse import mybir as _mybir
    from concourse.bass_utils import run_bass_kernel_spmd as _run

    nc = _bacc.Bacc("TRN2", target_bir_lowering=False, num_devices=1)
    arrays, args = {}, []
    for name in _INS:
        a = _np.ascontiguousarray(inputs[name])
        arrays[f"in_{name}_dram"] = a
        args.append(nc.dram_tensor(f"in_{name}_dram", a.shape, _mybir.dt.from_np(a.dtype), kind="ExternalInput").ap())
    shape = inputs['L0_attn_x'].shape
    args.append(nc.dram_tensor("out_0_dram", shape, _mybir.dt.float32, kind="ExternalOutput").ap())
    adaln_block(nc, *args)
    r = _run(nc, [arrays], core_ids=[0])
    return r.results[0]["out_0_dram"]
```
